# Optimizing a Trainium2 kernel written in Bass

```python
import numpy as np
import jax
import jax.numpy as jnp

def _softmax(x, axis=-1):
    return jax.nn.softmax(x, axis=axis)

def _gelu(x):
    return jax.nn.gelu(x, approximate=True)

def _silu(x):
    return jax.nn.silu(x)

def _sigmoid(x):
    return jax.nn.sigmoid(x)

def _layernorm(x, axis=-1, eps=1e-05):
    m = jnp.mean(x, axis=axis, keepdims=True)
    v = jnp.var(x, axis=axis, keepdims=True)
    return (x - m) / jnp.sqrt(v + eps)

def _scatter_add(tgt, idx, src, axis=0):
    return tgt.at[idx].add(src)

def _segment_sum(src, seg, n):
    return jax.ops.segment_sum(src, seg, n)
kernel_name = 'mk_cond_resid_d2_seqx_r2_a2378c'

def setup_inputs(seed: int=0):
    np.random.seed(seed)
    _w = jnp.asarray

    def _rec_inputs():
        import jax
        import jax.numpy as jnp
        _rk = jax.random.key(seed)
        x = -7.109e-05 + 0.9999 * jax.random.normal(jax.random.fold_in(_rk, 1), (128, 128, 2048), jnp.float32)
        _lenS = 128 - jax.random.randint(jax.random.fold_in(_rk, 7), (128,), 0, max(1, 128 // 4) + 1, jnp.int32)
        _lenS2 = 128 - jax.random.randint(jax.random.fold_in(_rk, 8), (128,), 0, max(1, 128 // 4) + 1, jnp.int32)
        itok_B_0_15 = jax.random.randint(jax.random.fold_in(_rk, 11), (128,), 0, 16, jnp.int32)
        itok_B_8_3872 = jax.random.randint(jax.random.fold_in(_rk, 12), (128,), 8, 3873, jnp.int32)
        return (x, itok_B_0_15, itok_B_8_3872)
    x, itok_B_0_15, itok_B_8_3872 = _rec_inputs()

    def _L0_cond_setup():
        import jax, jax.numpy as jnp
        import numpy as np
        NUM_CONDITIONS = 16
        IN_CH = 128
        OUT_CH = 128
        B = 64
        T = 2048
        key = jax.random.key(seed)
        k_x, k_w, k_c = jax.random.split(key, 3)
        x = jax.random.normal(k_x, (B, IN_CH, T), dtype=jnp.float32)
        bound = float(np.sqrt(6.0 / IN_CH))
        weights = jax.random.uniform(k_w, (NUM_CONDITIONS, IN_CH, OUT_CH), dtype=jnp.float32, minval=-bound, maxval=bound)
        condition = jax.random.randint(k_c, (B,), 0, NUM_CONDITIONS, dtype=jnp.int64)
        return {'x': x, 'weights': weights, 'condition': condition}
    _L0_cond_all = _L0_cond_setup()
    _L0_cond_in = {k: v for k, v in _L0_cond_all.items() if k in ('weights',)}
    del _L0_cond_all

    def _L1_cond_setup():
        import math
        import jax, jax.numpy as jnp
        import numpy as np
        H, N, B, L = (128, 64, 16, 2048)
        DT_MIN, DT_MAX = (0.001, 0.1)

        def _get_kernel(log_dt, C, log_A_real, A_imag, length):
            Cc = C[..., 0] + 1j * C[..., 1]
            dt = jnp.exp(log_dt)
            A = -jnp.exp(log_A_real) + 1j * A_imag
            dtA = A * dt[:, None]
            P = dtA[:, :, None] * jnp.arange(length, dtype=jnp.float32)
            Cs = Cc * (jnp.exp(dtA) - 1.0) / A
            K = 2.0 * jnp.einsum('hn,hnl->hl', Cs, jnp.exp(P)).real
            return K
        key = jax.random.key(seed)
        ks = jax.random.split(key, 6)
        u = jax.random.normal(ks[0], (B, H, L), dtype=jnp.float32)
        length = jax.random.randint(ks[1], (B,), 0, L)
        log_dt = jax.random.uniform(ks[2], (H,), dtype=jnp.float32) * (math.log(DT_MAX) - math.log(DT_MIN)) + math.log(DT_MIN)
        C = jax.random.normal(ks[3], (H, N, 2), dtype=jnp.float32)
        log_A_real = jnp.log(0.5 * jnp.ones((H, N), dtype=jnp.float32))
        A_imag = math.pi * jnp.broadcast_to(jnp.arange(N, dtype=jnp.float32), (H, N))
        D = jax.random.normal(ks[4], (H,), dtype=jnp.float32)
        return {'u': u, 'length': length, 'log_dt': log_dt, 'C': C, 'log_A_real': log_A_real, 'A_imag': A_imag, 'D': D}
    _L1_cond_all = _L1_cond_setup()
    _L1_cond_in = {k: v for k, v in _L1_cond_all.items() if k in ('log_dt', 'C', 'log_A_real', 'A_imag', 'D')}
    del _L1_cond_all
    return {'x': x, 'itok_B_0_15': itok_B_0_15, 'itok_B_8_3872': itok_B_8_3872, 'L0_cond_weights': _L0_cond_in['weights'], 'L1_cond_log_dt': _L1_cond_in['log_dt'], 'L1_cond_C': _L1_cond_in['C'], 'L1_cond_log_A_real': _L1_cond_in['log_A_real'], 'L1_cond_A_imag': _L1_cond_in['A_imag'], 'L1_cond_D': _L1_cond_in['D']}

def reference(x, itok_B_0_15, itok_B_8_3872, L0_cond_weights, L1_cond_log_dt, L1_cond_C, L1_cond_log_A_real, L1_cond_A_imag, L1_cond_D):
    import jax
    import jax.numpy as jnp

    def _L0_cond_ref(x, weights, condition):
        import jax, jax.numpy as jnp
        import numpy as np
        NUM_CONDITIONS = 16
        IN_CH = 128
        OUT_CH = 128
        B = 64
        T = 2048
        W = weights[condition]
        return jnp.einsum('bct,bcd->bdt', x, W)

    def _L1_cond_ref(u, length, log_dt, C, log_A_real, A_imag, D):
        import math
        import jax, jax.numpy as jnp
        import numpy as np
        H, N, B, L = (128, 64, 16, 2048)
        DT_MIN, DT_MAX = (0.001, 0.1)

        def _get_kernel(log_dt, C, log_A_real, A_imag, length):
            Cc = C[..., 0] + 1j * C[..., 1]
            dt = jnp.exp(log_dt)
            A = -jnp.exp(log_A_real) + 1j * A_imag
            dtA = A * dt[:, None]
            P = dtA[:, :, None] * jnp.arange(length, dtype=jnp.float32)
            Cs = Cc * (jnp.exp(dtA) - 1.0) / A
            K = 2.0 * jnp.einsum('hn,hnl->hl', Cs, jnp.exp(P)).real
            return K
        Bq, Hq, Lq = u.shape
        mask = (jnp.arange(Lq) < length[:, None]).astype(u.dtype)
        u_m = u * mask[:, None, :]
        kernel = _get_kernel(log_dt, C, log_A_real, A_imag, Lq)
        n = 2 * Lq
        k_f = jnp.fft.rfft(kernel, n=n)
        u_f = jnp.fft.rfft(u_m, n=n)
        y = jnp.fft.irfft(u_f * k_f, n=n)[..., :Lq]
        y = y + u_m * D[:, None]
        return y * mask[:, None, :]
    x = x + _L0_cond_ref(x, L0_cond_weights, itok_B_0_15)
    x = x + _L1_cond_ref(x, itok_B_8_3872, L1_cond_log_dt, L1_cond_C, L1_cond_log_A_real, L1_cond_A_imag, L1_cond_D)
    return x

_drawn_inputs = setup_inputs


def setup_inputs(seed=0):
    import zlib

    import numpy as np

    out = dict(_drawn_inputs(seed))
    spreads = {'L1_cond_log_A_real': (-0.6931471824645996, 0.2)}
    factors = {}
    for name, (base, spread) in spreads.items():
        noise = np.random.default_rng([zlib.crc32(name.encode()), seed]).standard_normal(out[name].shape)
        drawn = base * np.exp(spread * noise) if base else spread * noise
        out[name] = jnp.asarray(drawn.astype(out[name].dtype))
    for name, factor in factors.items():
        out[name] = (out[name] * factor).astype(out[name].dtype)
    return out
```

```python
import concourse.bass as bass
from concourse import mybir
from contextlib import ExitStack

B, H, T = 128, 128, 2048
P = 128
N = 64
NCOND = 16
CHUNK = 256
NCH = T // CHUNK
NBLK = T // P
BANK = 512
NQ = T // BANK
SLOTS = 4
ROUND = 12582912.0
LOG2E = 1.4426950408889634
LN2 = (0.693359375, -2.12194440e-4)
TWO_PI = (6.28125, 1.9350051879882812e-3, 3.019915981956752e-7)
INV_2PI = 0.15915494309189535
SIN_SCALE = 6.283185
EXP_POLY = [1 / 5040, 1 / 720, 1 / 120, 1 / 24, 1 / 6, 0.5, 1.0, 1.0]
HIGH, LOW = 17, 16
NEXP = HIGH + LOW
NTRIG = 2 * NEXP
COL_P1, COL_P2, COL_Q1, COL_Q2 = 0, HIGH, 2 * HIGH, 2 * HIGH + LOW
COL_S1, COL_S2, COL_CK, COL_RD, COL_RO, COL_DP = range(NTRIG, NTRIG + 6)
NCOL = NTRIG + 6
HS = 32
C_EYE, C_SWAP, C_ONES, C_TAU, C_OFF, C_EXP, C_DELTA = 0, 128, 256, 384, 384 + NTRIG, 384 + 2 * NTRIG, 384 + 2 * NTRIG + NEXP
NCONST = C_DELTA + CHUNK


def s4d_program(nc, x, cond, length, weights, log_dt, c_in, log_a_real, a_imag, d_in, const_in, out):
    fp32, int32, uint8 = mybir.dt.float32, mybir.dt.int32, mybir.dt.uint8
    ALU = mybir.AluOpType
    ACT = mybir.ActivationFunctionType

    x1_dram = nc.dram_tensor("x1_scratch", (B, H, T), fp32, kind="Internal").ap()
    k_dram = [nc.dram_tensor(f"k_scratch{i}", (P, P + CHUNK), fp32, kind="Internal").ap() for i in range(2)]

    ctx = ExitStack()
    with ctx:
        def sb(name, shape, dt=fp32):
            return ctx.enter_context(nc.sbuf_tensor(name, shape, dt))

        def sem(name):
            return ctx.enter_context(nc.semaphore(name))

        tile = [sb(f"tile{i}", [P, T]) for i in range(SLOTS)]
        side = [sb(f"side{i}", [P, T]) for i in range(SLOTS)]
        u_t = [side[i][:, :].rearrange("s (k b) -> s k b", b=B) for i in range(2)]
        w_sel = [sb(f"w_sel{i}", [P, P]) for i in range(SLOTS)]
        const = sb("const", [P, NCONST])
        eye, swap = const[:, C_EYE:C_EYE + P], const[:, C_SWAP:C_SWAP + P]
        ones = const[:, C_ONES:C_ONES + P]
        tau, off = const[:, C_TAU:C_TAU + NTRIG], const[:, C_OFF:C_OFF + NTRIG]
        tau_exp, delta = const[:, C_EXP:C_EXP + NEXP], const[:, C_DELTA:C_DELTA + CHUNK]
        cond_sb = sb("cond_sb", [1, B], int32)
        len_i = sb("len_i", [P, 1], int32)
        len_f = sb("len_f", [P, 1])
        step_i = sb("step_i", [P, T], int32)
        mask = sb("mask", [P, T], uint8)
        table = sb("table", [P, H, NCOL])
        logs = sb("logs", [P, N + 1])
        aim = sb("aim", [P, N])
        c_sb = sb("c_sb", [P, N, 2])
        exps = sb("exps", [P, N + 1])
        base = sb("base", [P, 24, N])
        trig_arg = sb("trig_arg", [P, 2, N])
        trig_out = sb("trig_out", [P, 2, N])
        turned = sb("turned", [P, 5, P])
        ar_t = sb("ar_t", [P, H])
        f_t = sb("f_t", [P, H])
        d_bc = sb("d_bc", [P, H])
        ex = [sb(f"ex{i}", [P, HS * NEXP]) for i in range(5)]
        ex_i = sb("ex_i", [P, HS * NEXP], int32)
        tg = [sb(f"tg{i}", [P, HS, NTRIG]) for i in range(2)]
        par = [sb(f"par{i}", [P, NCOL]) for i in range(2)]
        outer = [sb(f"outer{i}", [P, 2, CHUNK]) for i in range(2)]
        e_mat = [sb(f"e_mat{i}", [P, CHUNK]) for i in range(2)]
        e_rev = [sb(f"e_rev{i}", [P, CHUNK]) for i in range(2)]
        m_tmp = [sb(f"m_tmp{i}", [P, P]) for i in range(2)]
        m_mat = [sb(f"m_mat{i}", [P, P]) for i in range(2)]
        r_tmp = [sb(f"r_tmp{i}", [P, P]) for i in range(2)]
        r_mat = [sb(f"r_mat{i}", [P, P]) for i in range(2)]
        ck_bc = [sb(f"ck_bc{i}", [P, P]) for i in range(2)]
        b_mat = [sb(f"b_mat{i}", [P, 2, P]) for i in range(2)]
        k_pad = [sb(f"k_pad{i}", [P, P + CHUNK]) for i in range(2)]
        toep = [sb(f"toep{i}", [P, CHUNK]) for i in range(2)]
        state = [sb(f"state{i}", [P, P]) for i in range(2)]

        bank = [ctx.enter_context(nc.psum_tensor(f"bank{i}", [P, BANK], fp32)) for i in range(8)]
        y_bank, t_bank, s_bank, b_bank, k_bank = bank[0:2], bank[2:4], bank[4:6], bank[6], bank[7]

        consts_in = sem("consts_in")
        pads_zeroed = sem("pads_zeroed")
        x_loaded = [sem(f"x_loaded{i}") for i in range(SLOTS)]
        w_loaded = [sem(f"w_loaded{i}") for i in range(SLOTS)]
        mixed = [sem(f"mixed{i}") for i in range(SLOTS)]
        x1_stored = [sem(f"x1_stored{i}") for i in range(SLOTS)]
        mm_done = sem("mm_done")
        dve_step = sem("dve_step")
        pool_step = sem("pool_step")
        steps_made = sem("steps_made")
        base_arg = sem("base_arg")
        base_trig = sem("base_trig")
        base_done = sem("base_done")
        turned_done = sem("turned_done")
        turned_kept = sem("turned_kept")
        sin_arg = sem("sin_arg")
        sin_done = sem("sin_done")
        x1_loaded = [sem(f"x1_loaded{i}") for i in range(SLOTS)]
        x2_stored = [sem(f"x2_stored{i}") for i in range(SLOTS)]
        par_ready = sem("par_ready")
        e_ready = sem("e_ready")
        mats_ready = sem("mats_ready")
        b_made = sem("b_made")
        b_ready = sem("b_ready")
        k_made = sem("k_made")
        k_ready = sem("k_ready")
        k_stored = [sem(f"k_stored{i}") for i in range(2)]
        toep_loaded = [sem(f"toep_loaded{i}") for i in range(2)]
        u_made = sem("u_made")
        u_ready = sem("u_ready")
        s_made = sem("s_made")
        s_ready = sem("s_ready")
        y_made = sem("y_made")
        y_seen = sem("y_seen")
        y_taken = sem("y_taken")

        def exp_steps(eng, link, dst, work, work_i):
            v, k, r, p = work
            link(eng.tensor_scalar(v, v, -87.0, 88.0, ALU.max, ALU.min))
            link(eng.tensor_scalar(k, v, LOG2E, ROUND, ALU.mult, ALU.add))
            link(eng.tensor_scalar(k, k, -ROUND, None, ALU.add))
            link(eng.tensor_scalar(r, k, -LN2[0], None, ALU.mult))
            link(eng.tensor_tensor(r, r, v, ALU.add))
            link(eng.tensor_scalar(v, k, -LN2[1], None, ALU.mult))
            link(eng.tensor_tensor(r, r, v, ALU.add))
            link(eng.tensor_scalar(work_i, k, 127.0, float(2 ** 23), ALU.add, ALU.mult))
            link(eng.tensor_scalar(p, r, EXP_POLY[0], EXP_POLY[1], ALU.mult, ALU.add))
            for c in EXP_POLY[2:]:
                link(eng.tensor_tensor(p, p, r, ALU.mult))
                link(eng.tensor_scalar(p, p, c, None, ALU.add))
            link(eng.tensor_tensor(dst, p, work_i.bitcast(fp32), ALU.mult))

        block = ctx.enter_context(nc.Block())

        NSETUP = 7

        @block.sync
        def _(sp):
            for dst, src in ((const[:, :], const_in),
                             (logs[:, 0:N], log_a_real), (logs[:, N:N + 1], log_dt.rearrange("(h a) -> h a", a=1)),
                             (aim[:, :], a_imag), (c_sb[:, :, :], c_in),
                             (len_i[:, :], length.rearrange("(b a) -> b a", a=1)),
                             (cond_sb[:, :], cond.rearrange("(a b) -> a b", a=1))):
                sp.dma_start(dst, src).then_inc(consts_in, 16)
            sp.dma_start(d_bc[:, :], d_in.rearrange("(a h) -> a h", a=1).to_broadcast([P, H])).then_inc(consts_in, 16)
            sp.wait_ge(consts_in, 16 * (NSETUP + 1))

            def load(b, g, j):
                if not (isinstance(g, int) and g == 0):
                    sp.wait_ge(mixed[j], g)
                sp.dma_start(tile[j][:, :], x[bass.ds(b, 1), :, :].rearrange("a c t -> (a c) t")).then_inc(x_loaded[j], 16)
                which = sp.value_load(cond_sb[0:1, bass.ds(b, 1)], min_val=0, max_val=NCOND - 1)
                sp.dma_start(w_sel[j][:, :], weights[bass.ds(which, 1), :, :].rearrange("a c d -> (a c) d")).then_inc(w_loaded[j], 16)

            def store(b, g, j):
                sp.wait_ge(mixed[j], g + 1)
                sp.dma_start(x1_dram[bass.ds(b, 1), :, :].rearrange("a c t -> (a c) t"), side[j][:, :]).then_inc(x1_stored[j], 16)

            def rows(g):
                for j in range(SLOTS):
                    load(g * SLOTS + j, g, j)
                    if j >= 2:
                        store(g * SLOTS + j - 2, g, j - 2)
                    elif not (isinstance(g, int) and g == 0):
                        store(g * SLOTS + j - 2, g - 1, j + 2)

            rows(0)
            with sp.Fori(1, B // SLOTS) as g:
                rows(g)
            for b in (B - 2, B - 1):
                store(b, B // SLOTS - 1, b % SLOTS)
            for j in range(SLOTS):
                sp.wait_ge(x1_stored[j], 16 * (B // SLOTS))

            def load_x1(h, g, j):
                if not (isinstance(g, int) and g == 0):
                    sp.wait_ge(x2_stored[j], 16 * g)
                sp.dma_start(tile[j][:, :], x1_dram[:, bass.ds(h, 1), :].rearrange("b a t -> b (a t)")).then_inc(x1_loaded[j], 16)

            def make_toeplitz(h, i, n):
                sp.wait_ge(k_ready, h + 1)
                sp.wait_ge(toep_loaded[i], 16 * n)
                sp.dma_start(k_dram[i], k_pad[i][:, :]).then_inc(k_stored[i], 16)
                sp.wait_ge(k_stored[i], 16 * (n + 1))
                skewed = bass.AP(tensor=k_dram[i].tensor, offset=k_dram[i].offset + P, ap=[[P + CHUNK - 1, P], [1, CHUNK]])
                sp.dma_start(toep[i][:, :], skewed).then_inc(toep_loaded[i], 16)

            def store_x2(h, g, j):
                sp.wait_ge(y_taken, NQ * (h + 1))
                sp.dma_start(out[:, bass.ds(h, 1), :].rearrange("b a t -> b (a t)"), tile[j][:, :]).then_inc(x2_stored[j], 16)

            sp.wait_ge(pads_zeroed, 2)
            load_x1(0, 0, 0)
            load_x1(1, 0, 1)
            make_toeplitz(0, 0, 0)

            def channels(g, loads, last):
                for j in range(SLOTS):
                    h = g * SLOTS + j
                    if j < 2:
                        load_x1(h + 2, g, j + 2)
                    elif not last:
                        load_x1(h + 2, g + 1, j - 2)
                    if not (last and j == SLOTS - 1):
                        make_toeplitz(h + 1, (j + 1) % 2, g * 2 + (j + 1) // 2)
                    store_x2(h, g, j)

            channels(0, True, False)
            with sp.Fori(1, H // SLOTS - 1) as g:
                channels(g, True, False)
            channels(H // SLOTS - 1, False, True)
            for j in range(SLOTS):
                sp.wait_ge(x2_stored[j], 16 * (H // SLOTS))

        @block.gpsimd
        def _(pool):
            done = [0]

            def link(ins):
                done[0] += 1
                ins.then_inc(pool_step, 1)
                pool.wait_ge(pool_step, done[0])

            for i in range(2):
                pool.memset(k_pad[i][:, 0:P], 0.0).then_inc(pads_zeroed, 1)
            pool.iota(step_i[:, :], [[1, T]], base=0, channel_multiplier=0).then_inc(steps_made, 1)
            pool.wait_ge(turned_kept, 2)
            pool.wait_ge(consts_in, 16 * (NSETUP + 1))

            def bc(ap, k):
                return ap.unsqueeze(2).to_broadcast([P, HS, k])

            for q in range(H // HS):
                hs = slice(q * HS, (q + 1) * HS)
                w, r = tg[0][:, :, :], tg[1][:, :, :]
                link(pool.tensor_tensor(w, bc(f_t[:, hs], NTRIG), tau.unsqueeze(1).to_broadcast([P, HS, NTRIG]), ALU.mult))
                for last in (False, True):
                    link(pool.tensor_scalar(r, w, ROUND, -ROUND, ALU.add, ALU.add))
                    if last:
                        link(pool.tensor_tensor(table[:, hs, 0:NTRIG], w, r, ALU.subtract))
                    else:
                        link(pool.tensor_tensor(w, w, r, ALU.subtract))
                        link(pool.tensor_tensor(w, w, off.unsqueeze(1).to_broadcast([P, HS, NTRIG]), ALU.add))
                pool.sem_inc(sin_arg, 1)
            for q in range(H // HS):
                hs = slice(q * HS, (q + 1) * HS)
                link(pool.tensor_tensor(ex[0][:, :].rearrange("p (h k) -> p h k", k=NEXP), bc(ar_t[:, hs], NEXP),
                                        tau_exp.unsqueeze(1).to_broadcast([P, HS, NEXP]), ALU.mult))
                exp_steps(pool, link, ex[4][:, :], [e[:, :] for e in ex[0:4]], ex_i[:, :])
                e = ex[4][:, :].rearrange("p (h k) -> p h k", k=NEXP)
                if q == 0:
                    pool.wait_ge(sin_done, 1)
                for col, k0, k in ((COL_P1, 0, HIGH), (COL_P2, 0, HIGH), (COL_Q1, HIGH, LOW), (COL_Q2, HIGH, LOW)):
                    link(pool.tensor_tensor(table[:, hs, col:col + k], table[:, hs, col:col + k], e[:, :, k0:k0 + k], ALU.mult))
            re, im, top = slice(0, N), slice(N, P), HIGH - 1
            link(pool.tensor_copy(table[re, :, COL_RD], table[re, :, COL_P1 + top]))
            link(pool.tensor_scalar(table[im, :, COL_RD], table[im, :, COL_P2 + top], -1.0, None, ALU.mult))
            link(pool.tensor_scalar(table[re, :, COL_RO], table[re, :, COL_P2 + top], -1.0, None, ALU.mult))
            link(pool.tensor_copy(table[im, :, COL_RO], table[im, :, COL_P1 + top]))
            link(pool.tensor_scalar(table[:, :, COL_DP], d_bc[:, :], 1.0, None, ALU.add))

            def make_e(h, i, first):
                if not first:
                    pool.wait_ge(y_made, NQ * (h - 1))
                    pool.wait_ge(k_made, h - 1)
                    pool.wait_ge(k_ready, h - 1)
                pool.tensor_copy(par[i][:, :], table[:, bass.ds(h, 1), :].rearrange("p a k -> p (a k)")).then_inc(par_ready, 1)
                pool.wait_ge(par_ready, h + 1)
                for n, (p0, q0) in enumerate(((COL_P1, COL_Q1), (COL_P2, COL_Q2))):
                    pool.tensor_tensor(outer[i][:, n, :].rearrange("p (a b) -> p a b", b=LOW),
                                       par[i][:, p0:p0 + LOW].unsqueeze(2).to_broadcast([P, LOW, LOW]),
                                       par[i][:, q0:q0 + LOW].unsqueeze(1).to_broadcast([P, LOW, LOW]),
                                       ALU.mult).then_inc(e_ready, 1)
                pool.wait_ge(e_ready, h * 4 + 2)
                pool.tensor_tensor(e_mat[i][:, :], outer[i][:, 0, :], outer[i][:, 1, :], ALU.add).then_inc(e_ready, 1)
                pool.tensor_tensor(e_rev[i][:, :], outer[i][:, 0, CHUNK - 1::-1], outer[i][:, 1, CHUNK - 1::-1], ALU.add).then_inc(e_ready, 1)

            for h in range(2):
                make_e(h, h, True)
            with pool.Fori(1, H // 2) as g:
                for i in range(2):
                    make_e(g * 2 + i, i, False)

        @block.scalar
        def _(act):
            act.wait_ge(base_arg, 1)
            nc.scalar.activation(trig_out[:, :, :], trig_arg[:, :, :], ACT.Sin, scale=SIN_SCALE).then_inc(base_trig, 1)
            act.wait_ge(turned_done, 5)
            for n, dst in enumerate((ar_t[:, :], f_t[:, :], table[:, :, COL_S1], table[:, :, COL_S2])):
                last = nc.scalar.activation(dst, bank[0][:, n * P:(n + 1) * P], ACT.Copy)
            last.then_inc(turned_kept, 1)
            nc.scalar.activation(table[:, :, COL_CK], bank[1][:, 0:P], ACT.Copy).then_inc(turned_kept, 1)
            act.wait_ge(sin_arg, H // HS)
            nc.scalar.activation(table[:, :, 0:NTRIG], table[:, :, 0:NTRIG], ACT.Sin, scale=SIN_SCALE).then_inc(sin_done, 1)

            def keep_b(h, i):
                act.wait_ge(b_made, h + 1)
                nc.scalar.activation(b_mat[i][:, :, :], b_bank[:, 0:2 * P].rearrange("p (a n) -> p a n", a=2), ACT.Copy).then_inc(b_ready, 1)

            def keep_u(h, i, q):
                act.wait_ge(u_made, h * NQ + (q + 1))
                nc.scalar.activation(side[i][:, q * BANK:(q + 1) * BANK], t_bank[q % 2][:, :], ACT.Copy).then_inc(u_ready, 1)

            def keep_s(h, c):
                act.wait_ge(s_made, h * (NCH - 1) + c)
                nc.scalar.activation(state[c % 2][:, :], s_bank[(c - 1) // 4][:, ((c - 1) % 4) * P:((c - 1) % 4 + 1) * P], ACT.Copy).then_inc(s_ready, 1)

            def channel(h, i, last):
                keep_s(h, 1)
                for c in range(1, NCH):
                    if c < NCH - 1:
                        keep_s(h, c + 1)
                    if not last:
                        if c % 2:
                            keep_u(h + 1, 1 - i, c // 2)
                        if c == 4:
                            keep_b(h + 1, 1 - i)

            for q in range(NQ):
                keep_u(0, 0, q)
            keep_b(0, 0)
            with act.Fori(0, H // 2 - 1) as g:
                for i in range(2):
                    channel(g * 2 + i, i, False)
            channel(H - 2, 0, False)
            channel(H - 1, 1, True)

        @block.vector
        def _(dve):
            done = [0]

            def link(ins):
                done[0] += 1
                ins.then_inc(dve_step, 1)
                dve.wait_ge(dve_step, done[0])

            v = nc.vector
            dve.wait_ge(consts_in, 16 * (NSETUP + 1))
            link(v.tensor_copy(len_f[:, :], len_i[:, :]))
            (are, ar, ai, k, r, t, er, xr, xi, nr, den, rd, qr, qi, c2r, c2i, lr, li, w0, w1, w2) = (base[:, n, :] for n in range(21))
            e5 = [e[:, 0:N + 1] for e in ex]
            link(v.tensor_copy(e5[0], logs[:, :]))
            exp_steps(v, link, exps[:, :], e5[0:4], ex_i[:, 0:N + 1])
            dt = exps[:, N:N + 1]
            link(v.tensor_scalar(are, exps[:, 0:N], -1.0, None, ALU.mult))
            link(v.tensor_scalar(ar, are, dt, None, ALU.mult))
            link(v.tensor_scalar(ai, aim[:, :], dt, None, ALU.mult))
            link(v.tensor_scalar(k, ai, INV_2PI, ROUND, ALU.mult, ALU.add))
            link(v.tensor_scalar(k, k, -ROUND, None, ALU.add))
            link(v.tensor_copy(r, ai))
            for part in TWO_PI:
                link(v.scalar_tensor_tensor(r, k, -part, r, ALU.mult, ALU.add))
            link(v.tensor_scalar(trig_arg[:, 0, :], r, INV_2PI, None, ALU.mult))
            link(v.tensor_scalar(w0, trig_arg[:, 0, :], 0.25, None, ALU.add))
            link(v.tensor_scalar(w1, w0, ROUND, -ROUND, ALU.add, ALU.add))
            v.tensor_tensor(trig_arg[:, 1, :], w0, w1, ALU.subtract).then_inc(base_arg, 1)
            e4 = [e[:, 0:N] for e in ex]
            link(v.tensor_copy(e4[0], ar))
            exp_steps(v, link, er, e4[0:4], ex_i[:, 0:N])
            dve.wait_ge(base_trig, 1)
            link(v.tensor_tensor(xr, er, trig_out[:, 1, :], ALU.mult))
            link(v.tensor_tensor(xi, er, trig_out[:, 0, :], ALU.mult))
            link(v.tensor_scalar(nr, xr, -1.0, None, ALU.add))
            link(v.tensor_tensor(w0, are, are, ALU.mult))
            link(v.tensor_tensor(w1, aim[:, :], aim[:, :], ALU.mult))
            link(v.tensor_tensor(den, w0, w1, ALU.add))
            link(v.reciprocal(rd, den))

            def complex_mult(o_re, o_im, a_re, a_im, b_re, b_im, conj=False):
                link(v.tensor_tensor(w0, a_re, b_re, ALU.mult))
                link(v.tensor_tensor(w1, a_im, b_im, ALU.mult))
                link(v.tensor_tensor(o_re, w0, w1, ALU.add if conj else ALU.subtract))
                link(v.tensor_tensor(w0, a_im, b_re, ALU.mult))
                link(v.tensor_tensor(w1, a_re, b_im, ALU.mult))
                link(v.tensor_tensor(o_im, w0, w1, ALU.subtract if conj else ALU.add))

            complex_mult(qr, qi, nr, xi, are, aim[:, :], conj=True)
            link(v.tensor_tensor(qr, qr, rd, ALU.mult))
            link(v.tensor_tensor(qi, qi, rd, ALU.mult))
            complex_mult(c2r, c2i, c_sb[:, :, 0], c_sb[:, :, 1], qr, qi)
            link(v.tensor_scalar(c2r, c2r, 2.0, None, ALU.mult))
            link(v.tensor_scalar(c2i, c2i, 2.0, None, ALU.mult))
            complex_mult(lr, li, c2r, c2i, xr, xi)
            for n, (one, two) in enumerate(((ar, ar), (trig_arg[:, 0, :], trig_arg[:, 0, :]), (lr, lr), (li, li), (c2r, c2i))):
                link(v.tensor_copy(turned[:, n, 0:N], one))
                if n == 2:
                    link(v.tensor_scalar(turned[:, n, N:P], two, -1.0, None, ALU.mult))
                elif n < 4:
                    link(v.tensor_copy(turned[:, n, N:P], two))
                else:
                    v.tensor_copy(turned[:, n, N:P], two).then_inc(base_done, 1)
            dve.wait_ge(steps_made, 1)
            link(v.tensor_scalar(mask[:, :], step_i[:, :], len_f[:, 0:1], None, ALU.is_lt))

            def mix(b, g, j):
                if not (isinstance(g, int) and g == 0):
                    dve.wait_ge(x1_stored[j], g * 16)
                dve.wait_ge(mm_done, b + 1)
                for q in range(NQ):
                    cols = slice(q * BANK, (q + 1) * BANK)
                    last = v.tensor_tensor(side[j][:, cols], bank[(j % 2) * NQ + q][:, :], tile[j][:, cols], ALU.add)
                last.then_inc(mixed[j], 1)

            for j in range(SLOTS):
                mix(j, 0, j)
            with dve.Fori(1, B // SLOTS) as g:
                for j in range(SLOTS):
                    mix(g * SLOTS + j, g, j)

            def mats(h, i):
                dve.wait_ge(par_ready, h + 1)
                if not (isinstance(h, int) and h < 2):
                    dve.wait_ge(y_made, NQ * (h - 1))
                p = par[i]
                v.tensor_scalar(m_tmp[i][:, :], eye, p[:, COL_S1:COL_S1 + 1], None, ALU.mult).then_inc(mats_ready, 1)
                v.tensor_scalar(r_tmp[i][:, :], eye, p[:, COL_RD:COL_RD + 1], None, ALU.mult).then_inc(mats_ready, 1)
                v.tensor_scalar(ck_bc[i][:, :], ones, p[:, COL_CK:COL_CK + 1], None, ALU.mult).then_inc(mats_ready, 1)
                dve.wait_ge(mats_ready, h * 5 + 3)
                v.scalar_tensor_tensor(m_mat[i][:, :], swap, p[:, COL_S2:COL_S2 + 1], m_tmp[i][:, :], ALU.mult, ALU.add).then_inc(mats_ready, 1)
                v.scalar_tensor_tensor(r_mat[i][:, :], swap, p[:, COL_RO:COL_RO + 1], r_tmp[i][:, :], ALU.mult, ALU.add).then_inc(mats_ready, 1)

            def keep_k(h, i, n):
                dve.wait_ge(k_made, h + 1)
                dve.wait_ge(k_stored[i], 16 * n)
                v.scalar_tensor_tensor(k_pad[i][:, P:P + CHUNK], delta, par[i][:, COL_DP:COL_DP + 1], k_bank[:, 0:CHUNK],
                                       ALU.mult, ALU.add).then_inc(k_ready, 1)

            def channel(h, i, j, n, last):
                if not last:
                    mats(h + 1, 1 - i)
                for q in range(NQ):
                    dve.wait_ge(y_made, h * NQ + (q + 1))
                    dve.sem_inc(y_seen, 1)
                    cols = slice(q * BANK, (q + 1) * BANK)
                    v.copy_predicated(tile[j][:, cols], mask[:, cols], y_bank[q % 2][:, :]).then_inc(y_taken, 1)
                    if q == 1 and not last:
                        keep_k(h + 1, 1 - i, n)

            dve.wait_ge(pads_zeroed, 2)
            mats(0, 0)
            keep_k(0, 0, 0)

            def channels(g, last):
                for j in range(SLOTS):
                    channel(g * SLOTS + j, j % 2, j, g * 2 + (j + 1) // 2, last and j == SLOTS - 1)

            channels(0, False)
            with dve.Fori(1, H // SLOTS - 1) as g:
                channels(g, False)
            channels(H // SLOTS - 1, True)

        @block.tensor
        def _(pe):
            mm = nc.tensor.matmul
            pe.wait_ge(consts_in, 16 * (NSETUP + 1))
            pe.wait_ge(base_done, 1)
            for n in range(5):
                nc.tensor.transpose(bank[n // 4][:, (n % 4) * P:(n % 4 + 1) * P], turned[:, n, :], eye).then_inc(turned_done, 1)
            pe.wait_ge(turned_kept, 2)

            def products(b, g, j):
                pe.wait_ge(x_loaded[j], (g + 1) * 16)
                pe.wait_ge(w_loaded[j], (g + 1) * 16)
                if not (isinstance(g, int) and g == 0 and j < 2):
                    pe.wait_ge(mixed[(j + 2) % SLOTS], g + 1 if j >= 2 else g)
                for q in range(NQ):
                    last = mm(bank[(j % 2) * NQ + q][:, :], w_sel[j][:, :], tile[j][:, q * BANK:(q + 1) * BANK], start=True, stop=True)
                last.then_inc(mm_done, 1)

            for j in range(SLOTS):
                products(j, 0, j)
            with pe.Fori(1, B // SLOTS) as g:
                for j in range(SLOTS):
                    products(g * SLOTS + j, g, j)
            for j in range(SLOTS):
                pe.wait_ge(mixed[j], B // SLOTS)

            def turn(h, j, k):
                q = k // 4
                if k % 4 == 0 and not (isinstance(h, int) and h == 0 and q < 2):
                    pe.wait_ge(u_ready, h * NQ + (q - 1))
                ins = nc.tensor.transpose(t_bank[q % 2][:, (k % 4) * P:(k % 4 + 1) * P], tile[j][:, k * P:(k + 1) * P], eye)
                if k % 4 == 3:
                    ins.then_inc(u_made, 1)

            def make_mats(h, i):
                pe.wait_ge(e_ready, h * 4 + 4)
                pe.wait_ge(mats_ready, h * 5 + 5)
                if not (isinstance(h, int) and h == 0):
                    pe.wait_ge(b_ready, h)
                    pe.wait_ge(k_ready, h)
                mm(k_bank[:, 0:CHUNK], ck_bc[i][:, :], e_mat[i][:, :], start=True, stop=True).then_inc(k_made, 1)
                for p in range(2):
                    ins = mm(b_bank[:, p * P:(p + 1) * P], e_rev[i][:, p * P:(p + 1) * P], m_mat[i][:, :], start=True, stop=True)
                ins.then_inc(b_made, 1)

            def drive(h, i, half):
                c0, n = (0, 4) if half == 0 else (4, NCH - 5)
                u = u_t[i].rearrange("s (c p) b -> s c p b", p=2)
                for p in range(2):
                    ins = mm(s_bank[half][:, 0:n * P], b_mat[i][:, p, :], u[:, c0:c0 + n, p, :], start=(p == 0), stop=(p == 1), skip_group_check=True)
                if half == 0:
                    ins.then_inc(s_made, 1)

            def channel(h, i, j, n, g, last):
                pe.wait_ge(b_ready, h + 1)
                pe.wait_ge(u_ready, h * NQ + NQ)
                drive(h, i, 0)
                if not last:
                    jn, gn = (j + 1) % SLOTS, g + (j + 1) // SLOTS
                    pe.wait_ge(x1_loaded[jn], (gn + 1) * 16)
                pe.wait_ge(toep_loaded[i], (n + 1) * 16)
                for c in range(NCH):
                    y = y_bank[(c // 2) % 2]
                    y0 = (c % 2) * CHUNK
                    if c >= 1:
                        pe.wait_ge(s_ready, h * (NCH - 1) + c)
                    if 1 <= c < NCH - 1:
                        at = (c % 4) * P
                        mm(s_bank[c // 4][:, at:at + P], r_mat[i][:, :], state[c % 2][:, :], start=False, stop=True, skip_group_check=True).then_inc(s_made, 1)
                    if c % 2 == 0 and not (isinstance(h, int) and h == 0 and c < 4):
                        pe.wait_ge(y_taken, h * NQ + (c // 2 - 1))
                    ins = mm(y[:, y0:y0 + CHUNK], u_t[i][:, 2 * c, :], toep[i][:, :], start=(c % 2 == 0), stop=False, skip_group_check=True)
                    ins = mm(y[:, y0 + P:y0 + CHUNK], u_t[i][:, 2 * c + 1, :], toep[i][:, 0:P], start=False, stop=(c == 0), skip_group_check=True)
                    if c >= 1:
                        ins = mm(y[:, y0:y0 + CHUNK], state[c % 2][:, :], e_mat[i][:, :], start=False, stop=True, skip_group_check=True)
                    if c % 2:
                        ins.then_inc(y_made, 1)
                    if c == 2:
                        drive(h, i, 1)
                    if not last:
                        turn(h + 1, jn, 2 * c)
                        turn(h + 1, jn, 2 * c + 1)
                        if c == 3:
                            make_mats(h + 1, 1 - i)

            pe.wait_ge(x1_loaded[0], 16)
            for k in range(NBLK):
                turn(0, 0, k)
            make_mats(0, 0)

            def channels(g, last):
                for j in range(SLOTS):
                    channel(g * SLOTS + j, j % 2, j, g * 2 + j // 2, g, last and j == SLOTS - 1)

            channels(0, False)
            with pe.Fori(1, H // SLOTS - 1) as g:
                channels(g, False)
            channels(H // SLOTS - 1, True)


_INS = ["x", "itok_B_0_15", "itok_B_8_3872", "L0_cond_weights", "L1_cond_log_dt", "L1_cond_C",
        "L1_cond_log_A_real", "L1_cond_A_imag", "L1_cond_D"]


def _constants(np):
    c = np.zeros((P, NCONST), np.float32)
    rows = np.arange(P)
    c[rows, C_EYE + rows] = 1.0
    c[rows, C_SWAP + (rows + N) % P] = 1.0
    c[:, C_ONES:C_ONES + P] = 1.0
    high, low = 16.0 * np.arange(HIGH), np.arange(LOW)
    c[:, C_TAU:C_TAU + NTRIG] = np.concatenate([high, high, low, low])
    imag = (rows >= N)[:, None] * 0.25
    o = np.concatenate([np.full(HIGH, 0.25), np.full(HIGH, 0.5), np.full(LOW, 0.25), np.zeros(LOW)])
    c[:, C_OFF:C_OFF + NTRIG] = o + imag * (np.arange(NTRIG) < 2 * HIGH)
    c[:, C_EXP:C_EXP + NEXP] = np.concatenate([high, low])
    c[:, C_DELTA] = 1.0
    return c


def kernel(**inputs):
    import numpy as np
    import concourse.bacc as bacc
    from concourse.bass_utils import run_bass_kernel_spmd

    nc = bacc.Bacc("TRN2", target_bir_lowering=False, num_devices=1)
    arrays, args = {}, []
    for name, a in [(n, np.ascontiguousarray(inputs[n])) for n in _INS] + [("constants", _constants(np))]:
        arrays[f"in_{name}"] = a
        args.append(nc.dram_tensor(f"in_{name}", a.shape, mybir.dt.from_np(a.dtype), kind="ExternalInput").ap())
    out = nc.dram_tensor("out_0", (B, H, T), mybir.dt.float32, kind="ExternalOutput").ap()
    s4d_program(nc, *args[:9], args[9], out)
    r = run_bass_kernel_spmd(nc, [arrays], core_ids=[0])
    return r.results[0]["out_0"]
```

```python
import concourse.bass as bass
from concourse import mybir
from contextlib import ExitStack

B, H, T = 128, 128, 2048
P = 128
N = 64
NCOND = 16
CHUNK = 256
NCH = T // CHUNK
NBLK = T // P
BANK = 512
NQ = T // BANK
SLOTS = 4
ROUND = 12582912.0
LOG2E = 1.4426950408889634
LN2 = (0.693359375, -2.12194440e-4)
TWO_PI = (6.28125, 1.9350051879882812e-3, 3.019915981956752e-7)
INV_2PI = 0.15915494309189535
SIN_SCALE = 6.283185
EXP_POLY = [1 / 5040, 1 / 720, 1 / 120, 1 / 24, 1 / 6, 0.5, 1.0, 1.0]
HIGH, LOW = 17, 16
NEXP = HIGH + LOW
NTRIG = 2 * NEXP
COL_P1, COL_P2, COL_Q1, COL_Q2 = 0, HIGH, 2 * HIGH, 2 * HIGH + LOW
COL_S1, COL_S2, COL_CK, COL_RD, COL_RO, COL_DP = range(NTRIG, NTRIG + 6)
NCOL = NTRIG + 6
HS = 16
C_EYE, C_SWAP, C_ONES, C_TAU, C_OFF, C_EXP, C_DELTA = 0, 128, 256, 384, 384 + NTRIG, 384 + 2 * NTRIG, 384 + 2 * NTRIG + NEXP
NCONST = C_DELTA + CHUNK


def s4d_program(nc, x, cond, length, weights, log_dt, c_in, log_a_real, a_imag, d_in, const_in, out):
    fp32, fp32r, int32, uint8 = mybir.dt.float32, mybir.dt.float32r, mybir.dt.int32, mybir.dt.uint8
    ALU = mybir.AluOpType
    ACT = mybir.ActivationFunctionType

    x1_dram = nc.dram_tensor("x1_scratch", (B, H, T), fp32, kind="Internal").ap()
    k_dram = [nc.dram_tensor(f"k_scratch{i}", (P, P + CHUNK), fp32, kind="Internal").ap() for i in range(2)]

    ctx = ExitStack()
    with ctx:
        def sb(name, shape, dt=fp32):
            return ctx.enter_context(nc.sbuf_tensor(name, shape, dt))

        def sem(name):
            return ctx.enter_context(nc.semaphore(name))

        tile = [sb(f"tile{i}", [P, T]) for i in range(SLOTS)]
        side = [sb(f"side{i}", [P, T]) for i in range(SLOTS)]
        u_hi = [sb(f"u_hi{i}", [P, NBLK, B], fp32r) for i in range(2)]
        u_lo = [sb(f"u_lo{i}", [P, NBLK, B], fp32r) for i in range(2)]
        u_odd = [side[i][:, 0:T // 2].rearrange("s (c b) -> s c b", b=B) for i in range(2)]
        w_sel = [sb(f"w_sel{i}", [P, P]) for i in range(SLOTS)]
        const = sb("const", [P, NCONST])
        eye, swap = const[:, C_EYE:C_EYE + P], const[:, C_SWAP:C_SWAP + P]
        ones = const[:, C_ONES:C_ONES + P]
        tau, off = const[:, C_TAU:C_TAU + NTRIG], const[:, C_OFF:C_OFF + NTRIG]
        tau_exp, delta = const[:, C_EXP:C_EXP + NEXP], const[:, C_DELTA:C_DELTA + CHUNK]
        cond_sb = sb("cond_sb", [1, B], int32)
        len_i = sb("len_i", [P, 1], int32)
        len_f = sb("len_f", [P, 1])
        step_i = side[0].bitcast(int32)
        mask = sb("mask", [P, T], uint8)
        table = sb("table", [P, H, NCOL])
        logs = sb("logs", [P, N + 1])
        aim = sb("aim", [P, N])
        c_sb = sb("c_sb", [P, N, 2])
        exps = sb("exps", [P, N + 1])
        base = sb("base", [P, 24, N])
        trig_arg = sb("trig_arg", [P, 2, N])
        trig_out = sb("trig_out", [P, 2, N])
        turned = sb("turned", [P, 5, P])
        ar_t = sb("ar_t", [P, H])
        f_t = sb("f_t", [P, H])
        d_bc = sb("d_bc", [P, H])
        ex = [sb(f"ex{i}", [P, HS * NEXP]) for i in range(5)]
        ex_i = sb("ex_i", [P, HS * NEXP], int32)
        tg = [sb(f"tg{i}", [P, HS, NTRIG]) for i in range(2)]
        par = [sb(f"par{i}", [P, NCOL]) for i in range(2)]
        outer = [sb(f"outer{i}", [P, 2, CHUNK]) for i in range(2)]
        e_mat = [sb(f"e_mat{i}", [P, CHUNK]) for i in range(2)]
        e_rev = [sb(f"e_rev{i}", [P, CHUNK]) for i in range(2)]
        m_tmp = [sb(f"m_tmp{i}", [P, P]) for i in range(2)]
        m_mat = [sb(f"m_mat{i}", [P, P]) for i in range(2)]
        r_tmp = [sb(f"r_tmp{i}", [P, P]) for i in range(2)]
        r_mat = [sb(f"r_mat{i}", [P, P]) for i in range(2)]
        ck_bc = [sb(f"ck_bc{i}", [P, P]) for i in range(2)]
        e_hi = [sb(f"e_hi{i}", [P, CHUNK], fp32r) for i in range(2)]
        e_lo = [sb(f"e_lo{i}", [P, CHUNK], fp32r) for i in range(2)]
        b_hi = [sb(f"b_hi{i}", [P, 2, P], fp32r) for i in range(2)]
        b_lo = [sb(f"b_lo{i}", [P, 2, P], fp32r) for i in range(2)]
        t_hi = [sb(f"t_hi{i}", [P, CHUNK], fp32r) for i in range(2)]
        t_lo = [sb(f"t_lo{i}", [P, CHUNK], fp32r) for i in range(2)]
        k_pad = [sb(f"k_pad{i}", [P, P + CHUNK]) for i in range(2)]
        toep = [sb(f"toep{i}", [P, CHUNK]) for i in range(2)]
        state = [sb(f"state{i}", [P, P]) for i in range(3)]
        s_hi = [sb(f"s_hi{i}", [P, P], fp32r) for i in range(3)]
        s_lo = [sb(f"s_lo{i}", [P, P], fp32r) for i in range(3)]

        bank = [ctx.enter_context(nc.psum_tensor(f"bank{i}", [P, BANK], fp32)) for i in range(8)]
        y_bank, t_bank, s_bank, b_bank, k_bank = bank[0:2], bank[2:4], bank[4:6], bank[6], bank[7]

        consts_in = sem("consts_in")
        pads_zeroed = sem("pads_zeroed")
        x_loaded = [sem(f"x_loaded{i}") for i in range(SLOTS)]
        w_loaded = [sem(f"w_loaded{i}") for i in range(SLOTS)]
        mixed = [sem(f"mixed{i}") for i in range(SLOTS)]
        x1_stored = [sem(f"x1_stored{i}") for i in range(SLOTS)]
        mm_done = sem("mm_done")
        dve_step = sem("dve_step")
        pool_step = sem("pool_step")
        steps_made = sem("steps_made")
        base_arg = sem("base_arg")
        base_trig = sem("base_trig")
        base_done = sem("base_done")
        turned_done = sem("turned_done")
        turned_kept = sem("turned_kept")
        sin_arg = sem("sin_arg")
        sin_done = sem("sin_done")
        x1_loaded = [sem(f"x1_loaded{i}") for i in range(SLOTS)]
        x2_stored = [sem(f"x2_stored{i}") for i in range(SLOTS)]
        par_ready = sem("par_ready")
        e_ready = sem("e_ready")
        mats_ready = sem("mats_ready")
        b_made = sem("b_made")
        b_half = sem("b_half")
        b_ready = sem("b_ready")
        k_made = sem("k_made")
        k_ready = sem("k_ready")
        k_stored = [sem(f"k_stored{i}") for i in range(2)]
        toep_loaded = [sem(f"toep_loaded{i}") for i in range(2)]
        u_made = sem("u_made")
        u_half = sem("u_half")
        u_ready = sem("u_ready")
        s_made = sem("s_made")
        s_ready = sem("s_ready")
        s_half = sem("s_half")
        s_split = sem("s_split")
        toep_split = sem("toep_split")
        y_made = sem("y_made")
        y_seen = sem("y_seen")
        y_taken = sem("y_taken")

        def exp_steps(eng, link, dst, work, work_i):
            v, k, r, p = work
            link(eng.tensor_scalar(v, v, -87.0, 88.0, ALU.max, ALU.min))
            link(eng.tensor_scalar(k, v, LOG2E, ROUND, ALU.mult, ALU.add))
            link(eng.tensor_scalar(k, k, -ROUND, None, ALU.add))
            link(eng.tensor_scalar(r, k, -LN2[0], None, ALU.mult))
            link(eng.tensor_tensor(r, r, v, ALU.add))
            link(eng.tensor_scalar(v, k, -LN2[1], None, ALU.mult))
            link(eng.tensor_tensor(r, r, v, ALU.add))
            link(eng.tensor_scalar(work_i, k, 127.0, float(2 ** 23), ALU.add, ALU.mult))
            link(eng.tensor_scalar(p, r, EXP_POLY[0], EXP_POLY[1], ALU.mult, ALU.add))
            for c in EXP_POLY[2:]:
                link(eng.tensor_tensor(p, p, r, ALU.mult))
                link(eng.tensor_scalar(p, p, c, None, ALU.add))
            link(eng.tensor_tensor(dst, p, work_i.bitcast(fp32), ALU.mult))

        block = ctx.enter_context(nc.Block())

        NSETUP = 7

        @block.sync
        def _(sp):
            for dst, src in ((const[:, :], const_in),
                             (logs[:, 0:N], log_a_real), (logs[:, N:N + 1], log_dt.rearrange("(h a) -> h a", a=1)),
                             (aim[:, :], a_imag), (c_sb[:, :, :], c_in),
                             (len_i[:, :], length.rearrange("(b a) -> b a", a=1)),
                             (cond_sb[:, :], cond.rearrange("(a b) -> a b", a=1))):
                sp.dma_start(dst, src).then_inc(consts_in, 16)
            sp.dma_start(d_bc[:, :], d_in.rearrange("(a h) -> a h", a=1).to_broadcast([P, H])).then_inc(consts_in, 16)
            sp.wait_ge(consts_in, 16 * (NSETUP + 1))

            def load(b, g, j):
                if not (isinstance(g, int) and g == 0):
                    sp.wait_ge(mixed[j], g)
                sp.dma_start(tile[j][:, :], x[bass.ds(b, 1), :, :].rearrange("a c t -> (a c) t")).then_inc(x_loaded[j], 16)
                which = sp.value_load(cond_sb[0:1, bass.ds(b, 1)], min_val=0, max_val=NCOND - 1)
                sp.dma_start(w_sel[j][:, :], weights[bass.ds(which, 1), :, :].rearrange("a c d -> (a c) d")).then_inc(w_loaded[j], 16)

            def store(b, g, j):
                sp.wait_ge(mixed[j], g + 1)
                sp.dma_start(x1_dram[bass.ds(b, 1), :, :].rearrange("a c t -> (a c) t"), side[j][:, :]).then_inc(x1_stored[j], 16)

            def rows(g):
                for j in range(SLOTS):
                    load(g * SLOTS + j, g, j)
                    if j >= 2:
                        store(g * SLOTS + j - 2, g, j - 2)
                    elif not (isinstance(g, int) and g == 0):
                        store(g * SLOTS + j - 2, g - 1, j + 2)

            rows(0)
            with sp.Fori(1, B // SLOTS) as g:
                rows(g)
            for b in (B - 2, B - 1):
                store(b, B // SLOTS - 1, b % SLOTS)
            for j in range(SLOTS):
                sp.wait_ge(x1_stored[j], 16 * (B // SLOTS))

            def load_x1(h, g, j):
                if not (isinstance(g, int) and g == 0):
                    sp.wait_ge(x2_stored[j], 16 * g)
                sp.dma_start(tile[j][:, :], x1_dram[:, bass.ds(h, 1), :].rearrange("b a t -> b (a t)")).then_inc(x1_loaded[j], 16)

            def make_toeplitz(h, i, n):
                sp.wait_ge(k_ready, h + 1)
                sp.wait_ge(toep_loaded[i], 16 * n)
                sp.dma_start(k_dram[i], k_pad[i][:, :]).then_inc(k_stored[i], 16)
                sp.wait_ge(k_stored[i], 16 * (n + 1))
                skewed = bass.AP(tensor=k_dram[i].tensor, offset=k_dram[i].offset + P, ap=[[P + CHUNK - 1, P], [1, CHUNK]])
                sp.dma_start(toep[i][:, :], skewed).then_inc(toep_loaded[i], 16)

            def store_x2(h, g, j):
                sp.wait_ge(y_taken, NQ * (h + 1))
                sp.dma_start(out[:, bass.ds(h, 1), :].rearrange("b a t -> b (a t)"), tile[j][:, :]).then_inc(x2_stored[j], 16)

            sp.wait_ge(pads_zeroed, 2)
            load_x1(0, 0, 0)
            load_x1(1, 0, 1)
            make_toeplitz(0, 0, 0)

            def channels(g, loads, last):
                for j in range(SLOTS):
                    h = g * SLOTS + j
                    if j < 2:
                        load_x1(h + 2, g, j + 2)
                    elif not last:
                        load_x1(h + 2, g + 1, j - 2)
                    if not (last and j == SLOTS - 1):
                        make_toeplitz(h + 1, (j + 1) % 2, g * 2 + (j + 1) // 2)
                    store_x2(h, g, j)

            channels(0, True, False)
            with sp.Fori(1, H // SLOTS - 1) as g:
                channels(g, True, False)
            channels(H // SLOTS - 1, False, True)
            for j in range(SLOTS):
                sp.wait_ge(x2_stored[j], 16 * (H // SLOTS))

        @block.gpsimd
        def _(pool):
            done = [0]

            def link(ins):
                done[0] += 1
                ins.then_inc(pool_step, 1)
                pool.wait_ge(pool_step, done[0])

            for i in range(2):
                pool.memset(k_pad[i][:, 0:P], 0.0).then_inc(pads_zeroed, 1)
            pool.iota(step_i[:, :], [[1, T]], base=0, channel_multiplier=0).then_inc(steps_made, 1)
            pool.wait_ge(turned_kept, 2)
            pool.wait_ge(consts_in, 16 * (NSETUP + 1))

            def bc(ap, k):
                return ap.unsqueeze(2).to_broadcast([P, HS, k])

            for q in range(H // HS):
                hs = slice(q * HS, (q + 1) * HS)
                w, r = tg[0][:, :, :], tg[1][:, :, :]
                link(pool.tensor_tensor(w, bc(f_t[:, hs], NTRIG), tau.unsqueeze(1).to_broadcast([P, HS, NTRIG]), ALU.mult))
                for last in (False, True):
                    link(pool.tensor_scalar(r, w, ROUND, -ROUND, ALU.add, ALU.add))
                    if last:
                        link(pool.tensor_tensor(table[:, hs, 0:NTRIG], w, r, ALU.subtract))
                    else:
                        link(pool.tensor_tensor(w, w, r, ALU.subtract))
                        link(pool.tensor_tensor(w, w, off.unsqueeze(1).to_broadcast([P, HS, NTRIG]), ALU.add))
                pool.sem_inc(sin_arg, 1)
            for q in range(H // HS):
                hs = slice(q * HS, (q + 1) * HS)
                link(pool.tensor_tensor(ex[0][:, :].rearrange("p (h k) -> p h k", k=NEXP), bc(ar_t[:, hs], NEXP),
                                        tau_exp.unsqueeze(1).to_broadcast([P, HS, NEXP]), ALU.mult))
                exp_steps(pool, link, ex[4][:, :], [e[:, :] for e in ex[0:4]], ex_i[:, :])
                e = ex[4][:, :].rearrange("p (h k) -> p h k", k=NEXP)
                if q == 0:
                    pool.wait_ge(sin_done, 1)
                for col, k0, k in ((COL_P1, 0, HIGH), (COL_P2, 0, HIGH), (COL_Q1, HIGH, LOW), (COL_Q2, HIGH, LOW)):
                    link(pool.tensor_tensor(table[:, hs, col:col + k], table[:, hs, col:col + k], e[:, :, k0:k0 + k], ALU.mult))
            re, im, top = slice(0, N), slice(N, P), HIGH - 1
            link(pool.tensor_copy(table[re, :, COL_RD], table[re, :, COL_P1 + top]))
            link(pool.tensor_scalar(table[im, :, COL_RD], table[im, :, COL_P2 + top], -1.0, None, ALU.mult))
            link(pool.tensor_scalar(table[re, :, COL_RO], table[re, :, COL_P2 + top], -1.0, None, ALU.mult))
            link(pool.tensor_copy(table[im, :, COL_RO], table[im, :, COL_P1 + top]))
            link(pool.tensor_scalar(table[:, :, COL_DP], d_bc[:, :], 1.0, None, ALU.add))

            def make_e(h, i, first):
                if not first:
                    pool.wait_ge(y_made, NQ * (h - 1))
                    pool.wait_ge(k_made, h - 1)
                    pool.wait_ge(k_ready, h - 1)
                pool.tensor_copy(par[i][:, :], table[:, bass.ds(h, 1), :].rearrange("p a k -> p (a k)")).then_inc(par_ready, 1)
                pool.wait_ge(par_ready, h + 1)
                for n, (p0, q0) in enumerate(((COL_P1, COL_Q1), (COL_P2, COL_Q2))):
                    pool.tensor_tensor(outer[i][:, n, :].rearrange("p (a b) -> p a b", b=LOW),
                                       par[i][:, p0:p0 + LOW].unsqueeze(2).to_broadcast([P, LOW, LOW]),
                                       par[i][:, q0:q0 + LOW].unsqueeze(1).to_broadcast([P, LOW, LOW]),
                                       ALU.mult).then_inc(e_ready, 1)
                pool.wait_ge(e_ready, h * 6 + 2)
                pool.tensor_tensor(e_mat[i][:, :], outer[i][:, 0, :], outer[i][:, 1, :], ALU.add).then_inc(e_ready, 1)
                pool.tensor_tensor(e_hi[i][:, :], outer[i][:, 0, :], outer[i][:, 1, :], ALU.add).then_inc(e_ready, 1)
                pool.tensor_tensor(e_rev[i][:, :], outer[i][:, 0, CHUNK - 1::-1], outer[i][:, 1, CHUNK - 1::-1], ALU.add).then_inc(e_ready, 1)
                pool.wait_ge(e_ready, h * 6 + 4)
                pool.tensor_tensor(e_lo[i][:, :], e_mat[i][:, :], e_hi[i][:, :].bitcast(fp32), ALU.subtract).then_inc(e_ready, 1)

            for h in range(2):
                make_e(h, h, True)
            with pool.Fori(1, H // 2) as g:
                for i in range(2):
                    make_e(g * 2 + i, i, False)

        @block.scalar
        def _(act):
            act.wait_ge(base_arg, 1)
            nc.scalar.activation(trig_out[:, :, :], trig_arg[:, :, :], ACT.Sin, scale=SIN_SCALE).then_inc(base_trig, 1)
            act.wait_ge(turned_done, 5)
            for n, dst in enumerate((ar_t[:, :], f_t[:, :], table[:, :, COL_S1], table[:, :, COL_S2])):
                last = nc.scalar.activation(dst, bank[0][:, n * P:(n + 1) * P], ACT.Copy)
            last.then_inc(turned_kept, 1)
            nc.scalar.activation(table[:, :, COL_CK], bank[1][:, 0:P], ACT.Copy).then_inc(turned_kept, 1)
            act.wait_ge(sin_arg, H // HS)
            nc.scalar.activation(table[:, :, 0:NTRIG], table[:, :, 0:NTRIG], ACT.Sin, scale=SIN_SCALE).then_inc(sin_done, 1)

            def keep_b(h, i):
                act.wait_ge(b_made, h + 1)
                nc.scalar.activation(b_hi[i][:, :, :], b_bank[:, 0:2 * P].rearrange("p (a n) -> p a n", a=2), ACT.Copy).then_inc(b_half, 1)

            def keep_u(h, i, q):
                act.wait_ge(u_made, h * NQ + (q + 1))
                blocks = t_bank[q % 2][:, :].rearrange("s (k b) -> s k b", b=B)
                nc.scalar.activation(u_odd[i][:, 2 * q:2 * q + 2, :], blocks[:, 1::2, :], ACT.Copy)
                nc.scalar.activation(u_hi[i][:, 4 * q:4 * q + 4, :], blocks, ACT.Copy).then_inc(u_half, 1)

            def keep_s(h, c):
                act.wait_ge(s_made, h * (NCH - 1) + c)
                now = s_bank[(c - 1) // 4][:, ((c - 1) % 4) * P:((c - 1) % 4 + 1) * P]
                nc.scalar.activation(state[c % 3][:, :], now, ACT.Copy).then_inc(s_ready, 1)
                act.wait_ge(s_ready, h * (NCH - 1) + c)
                nc.scalar.activation(s_hi[c % 3][:, :], state[c % 3][:, :], ACT.Copy).then_inc(s_half, 1)

            def channel(h, i, last):
                keep_s(h, 1)
                for c in range(1, NCH):
                    if c < NCH - 1:
                        keep_s(h, c + 1)
                    if not last:
                        if c % 2:
                            keep_u(h + 1, 1 - i, c // 2)
                        if c == 3:
                            keep_b(h + 1, 1 - i)

            for q in range(NQ):
                keep_u(0, 0, q)
            keep_b(0, 0)
            with act.Fori(0, H // 2 - 1) as g:
                for i in range(2):
                    channel(g * 2 + i, i, False)
            channel(H - 2, 0, False)
            channel(H - 1, 1, True)

        @block.vector
        def _(dve):
            done = [0]

            def link(ins):
                done[0] += 1
                ins.then_inc(dve_step, 1)
                dve.wait_ge(dve_step, done[0])

            v = nc.vector
            dve.wait_ge(consts_in, 16 * (NSETUP + 1))
            link(v.tensor_copy(len_f[:, :], len_i[:, :]))
            (are, ar, ai, k, r, t, er, xr, xi, nr, den, rd, qr, qi, c2r, c2i, lr, li, w0, w1, w2) = (base[:, n, :] for n in range(21))
            e5 = [e[:, 0:N + 1] for e in ex]
            link(v.tensor_copy(e5[0], logs[:, :]))
            exp_steps(v, link, exps[:, :], e5[0:4], ex_i[:, 0:N + 1])
            dt = exps[:, N:N + 1]
            link(v.tensor_scalar(are, exps[:, 0:N], -1.0, None, ALU.mult))
            link(v.tensor_scalar(ar, are, dt, None, ALU.mult))
            link(v.tensor_scalar(ai, aim[:, :], dt, None, ALU.mult))
            link(v.tensor_scalar(k, ai, INV_2PI, ROUND, ALU.mult, ALU.add))
            link(v.tensor_scalar(k, k, -ROUND, None, ALU.add))
            link(v.tensor_copy(r, ai))
            for part in TWO_PI:
                link(v.scalar_tensor_tensor(r, k, -part, r, ALU.mult, ALU.add))
            link(v.tensor_scalar(trig_arg[:, 0, :], r, INV_2PI, None, ALU.mult))
            link(v.tensor_scalar(w0, trig_arg[:, 0, :], 0.25, None, ALU.add))
            link(v.tensor_scalar(w1, w0, ROUND, -ROUND, ALU.add, ALU.add))
            v.tensor_tensor(trig_arg[:, 1, :], w0, w1, ALU.subtract).then_inc(base_arg, 1)
            e4 = [e[:, 0:N] for e in ex]
            link(v.tensor_copy(e4[0], ar))
            exp_steps(v, link, er, e4[0:4], ex_i[:, 0:N])
            dve.wait_ge(base_trig, 1)
            link(v.tensor_tensor(xr, er, trig_out[:, 1, :], ALU.mult))
            link(v.tensor_tensor(xi, er, trig_out[:, 0, :], ALU.mult))
            link(v.tensor_scalar(nr, xr, -1.0, None, ALU.add))
            link(v.tensor_tensor(w0, are, are, ALU.mult))
            link(v.tensor_tensor(w1, aim[:, :], aim[:, :], ALU.mult))
            link(v.tensor_tensor(den, w0, w1, ALU.add))
            link(v.reciprocal(rd, den))

            def complex_mult(o_re, o_im, a_re, a_im, b_re, b_im, conj=False):
                link(v.tensor_tensor(w0, a_re, b_re, ALU.mult))
                link(v.tensor_tensor(w1, a_im, b_im, ALU.mult))
                link(v.tensor_tensor(o_re, w0, w1, ALU.add if conj else ALU.subtract))
                link(v.tensor_tensor(w0, a_im, b_re, ALU.mult))
                link(v.tensor_tensor(w1, a_re, b_im, ALU.mult))
                link(v.tensor_tensor(o_im, w0, w1, ALU.subtract if conj else ALU.add))

            complex_mult(qr, qi, nr, xi, are, aim[:, :], conj=True)
            link(v.tensor_tensor(qr, qr, rd, ALU.mult))
            link(v.tensor_tensor(qi, qi, rd, ALU.mult))
            complex_mult(c2r, c2i, c_sb[:, :, 0], c_sb[:, :, 1], qr, qi)
            link(v.tensor_scalar(c2r, c2r, 2.0, None, ALU.mult))
            link(v.tensor_scalar(c2i, c2i, 2.0, None, ALU.mult))
            complex_mult(lr, li, c2r, c2i, xr, xi)
            for n, (one, two) in enumerate(((ar, ar), (trig_arg[:, 0, :], trig_arg[:, 0, :]), (lr, lr), (li, li), (c2r, c2i))):
                link(v.tensor_copy(turned[:, n, 0:N], one))
                if n == 2:
                    link(v.tensor_scalar(turned[:, n, N:P], two, -1.0, None, ALU.mult))
                elif n < 4:
                    link(v.tensor_copy(turned[:, n, N:P], two))
                else:
                    v.tensor_copy(turned[:, n, N:P], two).then_inc(base_done, 1)
            dve.wait_ge(steps_made, 1)
            link(v.tensor_scalar(mask[:, :], step_i[:, :], len_f[:, 0:1], None, ALU.is_lt))

            def mix(b, g, j):
                if not (isinstance(g, int) and g == 0):
                    dve.wait_ge(x1_stored[j], g * 16)
                dve.wait_ge(mm_done, b + 1)
                for q in range(NQ):
                    cols = slice(q * BANK, (q + 1) * BANK)
                    last = v.tensor_tensor(side[j][:, cols], bank[(j % 2) * NQ + q][:, :], tile[j][:, cols], ALU.add)
                last.then_inc(mixed[j], 1)

            for j in range(SLOTS):
                mix(j, 0, j)
            with dve.Fori(1, B // SLOTS) as g:
                for j in range(SLOTS):
                    mix(g * SLOTS + j, g, j)

            def mats(h, i):
                dve.wait_ge(par_ready, h + 1)
                if not (isinstance(h, int) and h < 2):
                    dve.wait_ge(y_made, NQ * (h - 1))
                p = par[i]
                v.tensor_scalar(m_tmp[i][:, :], eye, p[:, COL_S1:COL_S1 + 1], None, ALU.mult).then_inc(mats_ready, 1)
                v.tensor_scalar(r_tmp[i][:, :], eye, p[:, COL_RD:COL_RD + 1], None, ALU.mult).then_inc(mats_ready, 1)
                v.tensor_scalar(ck_bc[i][:, :], ones, p[:, COL_CK:COL_CK + 1], None, ALU.mult).then_inc(mats_ready, 1)
                dve.wait_ge(mats_ready, h * 5 + 3)
                v.scalar_tensor_tensor(m_mat[i][:, :], swap, p[:, COL_S2:COL_S2 + 1], m_tmp[i][:, :], ALU.mult, ALU.add).then_inc(mats_ready, 1)
                v.scalar_tensor_tensor(r_mat[i][:, :], swap, p[:, COL_RO:COL_RO + 1], r_tmp[i][:, :], ALU.mult, ALU.add).then_inc(mats_ready, 1)

            def keep_k(h, i, n):
                dve.wait_ge(k_made, h + 1)
                dve.wait_ge(k_stored[i], 16 * n)
                v.scalar_tensor_tensor(k_pad[i][:, P:P + CHUNK], delta, par[i][:, COL_DP:COL_DP + 1], k_bank[:, 0:CHUNK],
                                       ALU.mult, ALU.add).then_inc(k_ready, 1)

            def split_b(h, i):
                dve.wait_ge(b_half, h + 1)
                v.tensor_tensor(b_lo[i][:, :, :], b_bank[:, 0:2 * P].rearrange("p (a n) -> p a n", a=2),
                                b_hi[i][:, :, :].bitcast(fp32), ALU.subtract).then_inc(b_ready, 1)

            def split_u(h, i, q):
                dve.wait_ge(u_half, h * NQ + (q + 1))
                v.tensor_tensor(u_lo[i][:, 4 * q:4 * q + 4, :], t_bank[q % 2][:, :].rearrange("s (k b) -> s k b", b=B),
                                u_hi[i][:, 4 * q:4 * q + 4, :].bitcast(fp32), ALU.subtract).then_inc(u_ready, 1)

            def split_s(h, c):
                dve.wait_ge(s_half, h * (NCH - 1) + c)
                v.tensor_tensor(s_lo[c % 3][:, :], state[c % 3][:, :], s_hi[c % 3][:, :].bitcast(fp32), ALU.subtract).then_inc(s_split, 1)

            def split_toeplitz(h, i, n):
                dve.wait_ge(toep_loaded[i], (n + 1) * 16)
                v.tensor_copy(t_hi[i][:, :], toep[i][:, :]).then_inc(toep_split, 1)
                dve.wait_ge(toep_split, h * 2 + 1)
                v.tensor_tensor(t_lo[i][:, :], toep[i][:, :], t_hi[i][:, :].bitcast(fp32), ALU.subtract).then_inc(toep_split, 1)

            def take_y(h, j, q):
                dve.wait_ge(y_made, h * NQ + (q + 1))
                dve.sem_inc(y_seen, 1)
                cols = slice(q * BANK, (q + 1) * BANK)
                v.copy_predicated(tile[j][:, cols], mask[:, cols], y_bank[q % 2][:, :]).then_inc(y_taken, 1)

            def channel(h, i, j, n, last):
                if not last:
                    mats(h + 1, 1 - i)
                split_s(h, 1)
                for c in range(1, NCH):
                    if c < NCH - 1:
                        split_s(h, c + 1)
                    if c % 2 == 0:
                        take_y(h, j, c // 2 - 1)
                    elif not last and c < NCH - 1:
                        split_u(h + 1, 1 - i, c // 2)
                    if not last and c == 3:
                        keep_k(h + 1, 1 - i, n)
                        split_b(h + 1, 1 - i)
                take_y(h, j, NQ - 1)
                if not last:
                    split_u(h + 1, 1 - i, NQ - 1)
                    split_toeplitz(h + 1, 1 - i, n)

            dve.wait_ge(pads_zeroed, 2)
            mats(0, 0)
            for q in range(NQ):
                split_u(0, 0, q)
            keep_k(0, 0, 0)
            split_b(0, 0)
            split_toeplitz(0, 0, 0)

            def channels(g, last):
                for j in range(SLOTS):
                    channel(g * SLOTS + j, j % 2, j, g * 2 + (j + 1) // 2, last and j == SLOTS - 1)

            channels(0, False)
            with dve.Fori(1, H // SLOTS - 1) as g:
                channels(g, False)
            channels(H // SLOTS - 1, True)

        @block.tensor
        def _(pe):
            mm = nc.tensor.matmul
            pe.wait_ge(consts_in, 16 * (NSETUP + 1))
            pe.wait_ge(base_done, 1)
            for n in range(5):
                nc.tensor.transpose(bank[n // 4][:, (n % 4) * P:(n % 4 + 1) * P], turned[:, n, :], eye).then_inc(turned_done, 1)
            pe.wait_ge(turned_kept, 2)

            def products(b, g, j):
                pe.wait_ge(x_loaded[j], (g + 1) * 16)
                pe.wait_ge(w_loaded[j], (g + 1) * 16)
                if not (isinstance(g, int) and g == 0 and j < 2):
                    pe.wait_ge(mixed[(j + 2) % SLOTS], g + 1 if j >= 2 else g)
                for q in range(NQ):
                    last = mm(bank[(j % 2) * NQ + q][:, :], w_sel[j][:, :], tile[j][:, q * BANK:(q + 1) * BANK], start=True, stop=True)
                last.then_inc(mm_done, 1)

            for j in range(SLOTS):
                products(j, 0, j)
            with pe.Fori(1, B // SLOTS) as g:
                for j in range(SLOTS):
                    products(g * SLOTS + j, g, j)
            for j in range(SLOTS):
                pe.wait_ge(mixed[j], B // SLOTS)

            def turn(h, j, k):
                q = k // 4
                if k % 4 == 0 and not (isinstance(h, int) and h == 0 and q < 2):
                    pe.wait_ge(u_ready, h * NQ + (q - 1))
                ins = nc.tensor.transpose(t_bank[q % 2][:, (k % 4) * P:(k % 4 + 1) * P], tile[j][:, k * P:(k + 1) * P], eye)
                if k % 4 == 3:
                    ins.then_inc(u_made, 1)

            def make_mats(h, i):
                pe.wait_ge(e_ready, h * 6 + 6)
                pe.wait_ge(mats_ready, h * 5 + 5)
                if not (isinstance(h, int) and h == 0):
                    pe.wait_ge(b_ready, h)
                    pe.wait_ge(k_ready, h)
                mm(k_bank[:, 0:CHUNK], ck_bc[i][:, :], e_mat[i][:, :], start=True, stop=True).then_inc(k_made, 1)
                for p in range(2):
                    ins = mm(b_bank[:, p * P:(p + 1) * P], e_rev[i][:, p * P:(p + 1) * P], m_mat[i][:, :], start=True, stop=True)
                ins.then_inc(b_made, 1)

            def split_mm(to, w_hi, w_lo, m_hi, m_lo, start, stop):
                mm(to, w_hi, m_hi, start=start, stop=False, skip_group_check=True)
                mm(to, w_hi, m_lo, start=False, stop=False, skip_group_check=True)
                return mm(to, w_lo, m_hi, start=False, stop=stop, skip_group_check=True)

            def drive(h, i, half):
                pe.wait_ge(u_ready, h * NQ + (2 * half + 2))
                c0, n = (0, 4) if half == 0 else (4, NCH - 5)
                u = [a[i][:, :, :].rearrange("s (c p) b -> s c p b", p=2)[:, c0:c0 + n, :, :] for a in (u_hi, u_lo)]
                for p in range(2):
                    ins = split_mm(s_bank[half][:, 0:n * P], b_hi[i][:, p, :], b_lo[i][:, p, :], u[0][:, :, p, :], u[1][:, :, p, :],
                                   start=(p == 0), stop=(p == 1))
                if half == 0:
                    ins.then_inc(s_made, 1)

            def channel(h, i, j, n, g, last):

                def place(c):
                    return y_bank[(c // 2) % 2], (c % 2) * CHUNK

                def from_state(c):
                    y, y0 = place(c)
                    pe.wait_ge(s_split, h * (NCH - 1) + c)
                    ins = split_mm(y[:, y0:y0 + CHUNK], s_hi[c % 3][:, :], s_lo[c % 3][:, :], e_hi[i][:, :], e_lo[i][:, :], start=False, stop=True)
                    if c % 2:
                        ins.then_inc(y_made, 1)

                pe.wait_ge(b_ready, h + 1)
                drive(h, i, 0)
                if not last:
                    jn, gn = (j + 1) % SLOTS, g + (j + 1) // SLOTS
                    pe.wait_ge(x1_loaded[jn], (gn + 1) * 16)
                pe.wait_ge(toep_split, h * 2 + 2)
                for c in range(NCH):
                    if 1 <= c < NCH - 1:
                        at = (c % 4) * P
                        pe.wait_ge(s_ready, h * (NCH - 1) + c)
                        mm(s_bank[c // 4][:, at:at + P], r_mat[i][:, :], state[c % 3][:, :], start=False, stop=True, skip_group_check=True).then_inc(s_made, 1)
                    if c % 2 == 0 and not (isinstance(h, int) and h == 0 and c < 4):
                        pe.wait_ge(y_taken, h * NQ + (c // 2 - 1))
                    if c % 2 == 0 and c > 0:
                        pe.wait_ge(u_ready, h * NQ + (c // 2 + 1))
                    y, y0 = place(c)
                    split_mm(y[:, y0:y0 + CHUNK], u_hi[i][:, 2 * c, :], u_lo[i][:, 2 * c, :], t_hi[i][:, :], t_lo[i][:, :], start=(c % 2 == 0), stop=False)
                    mm(y[:, y0 + P:y0 + CHUNK], u_odd[i][:, c, :], toep[i][:, 0:P], start=False, stop=(c == 0), skip_group_check=True)
                    if c >= 2:
                        from_state(c - 1)
                    if c == NCH - 1:
                        from_state(c)
                    if c == 2:
                        drive(h, i, 1)
                    if not last:
                        turn(h + 1, jn, 2 * c)
                        turn(h + 1, jn, 2 * c + 1)
                        if c == 3:
                            make_mats(h + 1, 1 - i)

            pe.wait_ge(x1_loaded[0], 16)
            for k in range(NBLK):
                turn(0, 0, k)
            make_mats(0, 0)

            def channels(g, last):
                for j in range(SLOTS):
                    channel(g * SLOTS + j, j % 2, j, g * 2 + j // 2, g, last and j == SLOTS - 1)

            channels(0, False)
            with pe.Fori(1, H // SLOTS - 1) as g:
                channels(g, False)
            channels(H // SLOTS - 1, True)


_INS = ["x", "itok_B_0_15", "itok_B_8_3872", "L0_cond_weights", "L1_cond_log_dt", "L1_cond_C",
        "L1_cond_log_A_real", "L1_cond_A_imag", "L1_cond_D"]


def _constants(np):
    c = np.zeros((P, NCONST), np.float32)
    rows = np.arange(P)
    c[rows, C_EYE + rows] = 1.0
    c[rows, C_SWAP + (rows + N) % P] = 1.0
    c[:, C_ONES:C_ONES + P] = 1.0
    high, low = 16.0 * np.arange(HIGH), np.arange(LOW)
    c[:, C_TAU:C_TAU + NTRIG] = np.concatenate([high, high, low, low])
    imag = (rows >= N)[:, None] * 0.25
    o = np.concatenate([np.full(HIGH, 0.25), np.full(HIGH, 0.5), np.full(LOW, 0.25), np.zeros(LOW)])
    c[:, C_OFF:C_OFF + NTRIG] = o + imag * (np.arange(NTRIG) < 2 * HIGH)
    c[:, C_EXP:C_EXP + NEXP] = np.concatenate([high, low])
    c[:, C_DELTA] = 1.0
    return c


def kernel(**inputs):
    import numpy as np
    import concourse.bacc as bacc
    from concourse.bass_utils import run_bass_kernel_spmd

    nc = bacc.Bacc("TRN2", target_bir_lowering=False, num_devices=1)
    arrays, args = {}, []
    for name, a in [(n, np.ascontiguousarray(inputs[n])) for n in _INS] + [("constants", _constants(np))]:
        arrays[f"in_{name}"] = a
        args.append(nc.dram_tensor(f"in_{name}", a.shape, mybir.dt.from_np(a.dtype), kind="ExternalInput").ap())
    out = nc.dram_tensor("out_0", (B, H, T), mybir.dt.float32, kind="ExternalOutput").ap()
    s4d_program(nc, *args[:9], args[9], out)
    r = run_bass_kernel_spmd(nc, [arrays], core_ids=[0])
    return r.results[0]["out_0"]
```

```python
import concourse.bass as bass
from concourse import mybir
from contextlib import ExitStack

B, H, T = 128, 128, 2048
P = 128
N = 64
NCOND = 16
CHUNK = 256
NSEG = 2
SEG = T // NSEG
NCH = SEG // CHUNK
NBLK = SEG // P
BANK = 512
NQ = SEG // BANK
SLOTS = 4
GROUPS = H // SLOTS
AHEAD = 4
ROWS_FIRST = B + AHEAD
SETUP = 2, 4, 19, 20, 28, 29
ROW_GROUPS = (B - AHEAD) // SLOTS
PAD = 1024
TOEP = P * (P + CHUNK)
ROUND = 12582912.0
LOG2E = 1.4426950408889634
LN2 = (0.693359375, -2.12194440e-4)
TWO_PI = (6.28125, 1.9350051879882812e-3, 3.019915981956752e-7)
INV_2PI = 0.15915494309189535
SIN_SCALE = 6.283185
EXP_POLY = [1 / 5040, 1 / 720, 1 / 120, 1 / 24, 1 / 6, 0.5, 1.0, 1.0]
HIGH, LOW = 17, 16
NEXP = HIGH + LOW
NTRIG = 2 * NEXP
COL_P1, COL_P2, COL_Q1, COL_Q2 = 0, HIGH, 2 * HIGH, 2 * HIGH + LOW
COL_S1, COL_S2, COL_CK, COL_RD, COL_RO, COL_DP = range(NTRIG, NTRIG + 6)
NCOL = NTRIG + 6
HS = 16
C_EYE, C_SWAP, C_ONES, C_TAU, C_OFF, C_EXP, C_DELTA = 0, 128, 256, 384, 384 + NTRIG, 384 + 2 * NTRIG, 384 + 2 * NTRIG + NEXP
NCONST = C_DELTA + CHUNK


def s4d_program(nc, x, cond, length, weights, log_dt, c_in, log_a_real, a_imag, d_in, const_in, out):
    fp32, fp32r, int32, uint8 = mybir.dt.float32, mybir.dt.float32r, mybir.dt.int32, mybir.dt.uint8
    ALU = mybir.AluOpType
    ACT = mybir.ActivationFunctionType

    x1_dram = [nc.dram_tensor(f"x1_scratch{i}", (B, H * SEG + PAD), fp32, kind="Internal").ap() for i in range(NSEG)]
    k_dram = nc.dram_tensor("k_scratch", (H, TOEP), fp32, kind="Internal").ap()
    b_dram = nc.dram_tensor("b_scratch", (H, P, 2 * P), fp32, kind="Internal").ap()
    edge_dram = nc.dram_tensor("edge_scratch", (H, P, B), fp32, kind="Internal").ap()

    ctx = ExitStack()
    with ctx:
        def sb(name, shape, dt=fp32):
            return ctx.enter_context(nc.sbuf_tensor(name, shape, dt))

        def sem(name):
            return ctx.enter_context(nc.semaphore(name))

        decay = sb("decay", [P, H, NEXP])
        decay_cols = decay[:, :, :].rearrange("p h k -> p (h k)")
        tile = [decay_cols[:, i * SEG:(i + 1) * SEG] for i in range(SLOTS)]
        row_x = [sb(f"row_x{i}", [P, SEG]) for i in range(SLOTS)]
        row_y = [sb(f"row_y{i}", [P, SEG]) for i in range(SLOTS)]
        u_hi = [sb(f"u_hi{i}", [P, NBLK, B], fp32r) for i in range(2)]
        u_lo = [sb(f"u_lo{i}", [P, NBLK, B], fp32r) for i in range(2)]
        u_odd = [sb(f"u_odd{i}", [P, NBLK // 2, B]) for i in range(2)]
        w_all = sb("w_all", [P, NCOND, P])
        w_sel = [sb(f"w_sel{i}", [P, P]) for i in range(SLOTS)]
        const = sb("const", [P, NCONST])
        eye, swap = const[:, C_EYE:C_EYE + P], const[:, C_SWAP:C_SWAP + P]
        ones = const[:, C_ONES:C_ONES + P]
        tau, off = const[:, C_TAU:C_TAU + NTRIG], const[:, C_OFF:C_OFF + NTRIG]
        tau_exp, delta = const[:, C_EXP:C_EXP + NEXP], const[:, C_DELTA:C_DELTA + CHUNK]
        cond_sb = sb("cond_sb", [1, NSEG * B], int32)
        len_i = sb("len_i", [P, 1], int32)
        len_f = sb("len_f", [P, 1])
        step_i = decay_cols[:, 0:T].bitcast(int32)
        mask = sb("mask", [P, T], uint8)
        table = sb("table", [P, H, NCOL])
        par = [sb(f"par{i}", [P, NCOL]) for i in range(SLOTS)]
        outer = sb("outer", [P, 2, CHUNK])
        e_mat = [sb(f"e_mat{i}", [P, CHUNK]) for i in range(SLOTS)]
        e_hi = [sb(f"e_hi{i}", [P, CHUNK], fp32r) for i in range(SLOTS)]
        e_lo = [sb(f"e_lo{i}", [P, CHUNK], fp32r) for i in range(SLOTS)]
        e_rev = [sb(f"e_rev{i}", [P, CHUNK]) for i in range(2)]
        m_tmp = [sb(f"m_tmp{i}", [P, P]) for i in range(2)]
        m_mat = [sb(f"m_mat{i}", [P, P]) for i in range(2)]
        r_tmp = [sb(f"r_tmp{i}", [P, P]) for i in range(2)]
        r_mat = [sb(f"r_mat{i}", [P, P]) for i in range(SLOTS)]
        ck_hi = [sb(f"ck_hi{i}", [P, P], fp32r) for i in range(2)]
        ck_lo = [sb(f"ck_lo{i}", [P, P], fp32r) for i in range(2)]
        b_hi = [sb(f"b_hi{i}", [P, 2, P], fp32r) for i in range(SLOTS)]
        b_lo = [sb(f"b_lo{i}", [P, 2, P], fp32r) for i in range(SLOTS)]
        k_pad = [sb(f"k_pad{i}", [P, P + CHUNK]) for i in range(2)]
        toep = [sb(f"toep{i}", [P, CHUNK]) for i in range(SLOTS)]
        t_hi = [sb(f"t_hi{i}", [P, CHUNK], fp32r) for i in range(SLOTS)]
        t_lo = [sb(f"t_lo{i}", [P, CHUNK], fp32r) for i in range(SLOTS)]
        state = [sb(f"state{i}", [P, P]) for i in range(NCH)]
        edge = [sb(f"edge{i}", [P, P]) for i in range(2)]
        s_hi = [sb(f"s_hi{i}", [P, P], fp32r) for i in range(NCH)]
        s_lo = [sb(f"s_lo{i}", [P, P], fp32r) for i in range(NCH)]

        set_up = ctx.enter_context(ExitStack())

        def early(name, shape):
            return set_up.enter_context(nc.sbuf_tensor(name, shape, fp32))

        logs = early("logs", [P, N + 1])
        aim = early("aim", [P, N])
        c_sb = early("c_sb", [P, N, 2])
        exps = early("exps", [P, N + 1])
        base = early("base", [P, 21, N])
        trig_arg = early("trig_arg", [P, 2, N])
        trig_out = early("trig_out", [P, 2, N])
        turned = early("turned", [P, 5, P])
        ar_t = early("ar_t", [P, H])
        f_t = early("f_t", [P, H])
        d_bc = early("d_bc", [P, H])
        ex_all = early("ex", [P, 5, HS * NEXP])
        ex, ex_i = [ex_all[:, i, :] for i in range(4)], ex_all[:, 4, :].bitcast(int32)
        tg = [early(f"tg{i}", [P, HS, NTRIG]) for i in range(2)]
        set_up.close()
        x_hi = [sb(f"x_hi{i}", [P, SEG], fp32r) for i in range(2)]
        x_lo = [sb(f"x_lo{i}", [P, SEG], fp32r) for i in range(2)]
        w_hi = [sb(f"w_hi{i}", [P, P], fp32r) for i in range(2)]
        w_lo = [sb(f"w_lo{i}", [P, P], fp32r) for i in range(2)]
        b_whole = [sb(f"b_whole{i}", [P, 2, P]) for i in range(2)]

        bank = [ctx.enter_context(nc.psum_tensor(f"bank{i}", [P, BANK], fp32)) for i in range(8)]
        y_bank, t_bank, s_bank, gen_bank, row_bank = bank[0:2], bank[2:4], bank[4:6], bank[6], bank[7]
        b_part = gen_bank[:, 0:CHUNK].rearrange("p (a n) -> p a n", a=2)
        k_part = gen_bank[:, CHUNK:2 * CHUNK]

        consts_in = sem("consts_in")
        pads_zeroed = sem("pads_zeroed")
        x_loaded = [sem(f"x_loaded{i}") for i in range(SLOTS)]
        w_in = sem("w_in")
        w_ready = sem("w_ready")
        w_picked = sem("w_picked")
        x1_stored = [sem(f"x1_stored{i}") for i in range(SLOTS)]
        row_halved = sem("row_halved")
        row_split = sem("row_split")
        row_made = sem("row_made")
        row_taken = sem("row_taken")
        dve_step = sem("dve_step")
        pool_step = sem("pool_step")
        steps_made = sem("steps_made")
        base_arg = sem("base_arg")
        base_trig = sem("base_trig")
        base_done = sem("base_done")
        turned_done = sem("turned_done")
        turned_kept = sem("turned_kept")
        sin_arg = sem("sin_arg")
        sin_done = sem("sin_done")
        decay_done = sem("decay_done")
        x1_loaded = [sem(f"x1_loaded{i}") for i in range(SLOTS)]
        x2_stored = [sem(f"x2_stored{i}") for i in range(SLOTS)]
        par_ready = sem("par_ready")
        e_ready = sem("e_ready")
        mats_ready = sem("mats_ready")
        gen_made = sem("gen_made")
        b_half = sem("b_half")
        b_stored = [sem(f"b_stored{i}") for i in range(2)]
        b_loaded = [sem(f"b_loaded{i}") for i in range(2)]
        b_ready = sem("b_ready")
        e_half = sem("e_half")
        e_split = sem("e_split")
        k_ready = sem("k_ready")
        k_stored = [sem(f"k_stored{i}") for i in range(2)]
        toep_loaded = [sem(f"toep_loaded{i}") for i in range(SLOTS)]
        toep_half = sem("toep_half")
        edge_saved = [sem(f"edge_saved{i}") for i in range(2)]
        edge_loaded = [sem(f"edge_loaded{i}") for i in range(2)]
        u_made = sem("u_made")
        u_half = sem("u_half")
        u_ready = sem("u_ready")
        s_made = sem("s_made")
        s_ready = sem("s_ready")
        s_half = sem("s_half")
        s_split = sem("s_split")
        toep_split = sem("toep_split")
        y_made = sem("y_made")
        y_seen = sem("y_seen")
        y_taken = sem("y_taken")

        def exp_steps(eng, link, dst, work, work_i):
            v, k, r, p = work
            link(eng.tensor_scalar(v, v, -87.0, 88.0, ALU.max, ALU.min))
            link(eng.tensor_scalar(k, v, LOG2E, ROUND, ALU.mult, ALU.add))
            link(eng.tensor_scalar(k, k, -ROUND, None, ALU.add))
            link(eng.tensor_scalar(r, k, -LN2[0], None, ALU.mult))
            link(eng.tensor_tensor(r, r, v, ALU.add))
            link(eng.tensor_scalar(v, k, -LN2[1], None, ALU.mult))
            link(eng.tensor_tensor(r, r, v, ALU.add))
            link(eng.tensor_scalar(work_i, k, 127.0, float(2 ** 23), ALU.add, ALU.mult))
            link(eng.tensor_scalar(p, r, EXP_POLY[0], EXP_POLY[1], ALU.mult, ALU.add))
            for c in EXP_POLY[2:]:
                link(eng.tensor_tensor(p, p, r, ALU.mult))
                link(eng.tensor_scalar(p, p, c, None, ALU.add))
            link(eng.tensor_tensor(dst, p, work_i.bitcast(fp32), ALU.mult))

        def row_groups(eng, group, *setup):
            group(0)
            for first, last, share in zip((1,) + SETUP, SETUP + (ROWS_FIRST // SLOTS,), setup + (None,)):
                with eng.Fori(first, last) as g:
                    group(g)
                if share:
                    share()

        def channel_groups(eng, group):
            group(0, 0, True)
            with eng.Fori(1, ROW_GROUPS - 1) as g:
                group(g, 0, True)
            group(ROW_GROUPS - 1, 0, True)
            for g in range(ROW_GROUPS, GROUPS):
                group(g, 0, False)
            with eng.Fori(GROUPS, NSEG * GROUPS - 1) as g:
                group(g, 1, False)
            group(NSEG * GROUPS - 1, 1, False)

        def later(g, j, seg, d):
            k, gd = g * SLOTS + (j + d), g + (j + d) // SLOTS
            if isinstance(g, int):
                if k >= NSEG * H:
                    return None
                seg = k // H
            return seg, k, gd

        def states_before(seg, k):
            return k * NCH if seg == 0 else k * (NCH - 1) + H

        def splits_before(seg, k):
            return k * (NCH - 1) if seg == 0 else k * NCH - H

        def mats_before(seg, k):
            return k * 6 if seg == 0 else k * 2 + 4 * H

        def e_before(seg, k):
            return k * 4 if seg == 0 else k * 3 + H

        block = ctx.enter_context(nc.Block())

        NSETUP = 7

        @block.sync
        def _(sp):
            sp.dma_start(const[:, :], const_in).then_inc(w_in, 16)
            sp.dma_start(w_all[:, :, :], weights.rearrange("k c d -> c k d")).then_inc(w_in, 16)
            for dst, src in ((cond_sb[:, 0:B], cond.rearrange("(a b) -> a b", a=1)),
                             (cond_sb[:, B:2 * B], cond.rearrange("(a b) -> a b", a=1)),
                             (logs[:, 0:N], log_a_real), (logs[:, N:N + 1], log_dt.rearrange("(h a) -> h a", a=1)),
                             (aim[:, :], a_imag), (c_sb[:, :, :], c_in),
                             (len_i[:, :], length.rearrange("(b a) -> b a", a=1))):
                sp.dma_start(dst, src).then_inc(consts_in, 16)
            sp.dma_start(d_bc[:, :], d_in.rearrange("(a h) -> a h", a=1).to_broadcast([P, H])).then_inc(consts_in, 16)

            def load_row(n, j, seg, b):
                if not (isinstance(n, int) and n < SLOTS):
                    sp.wait_ge(row_made, n * NQ - (SLOTS - 1) * NQ)
                sp.dma_start(row_x[j][:, :], x[bass.ds(b, 1), :, seg * SEG:(seg + 1) * SEG].rearrange("a c t -> (a c) t")).then_inc(x_loaded[j], 16)

            def store_row(n, j, seg, b):
                sp.wait_ge(row_taken, n * NQ + NQ)
                sp.dma_start(x1_dram[seg][bass.ds(b, 1), 0:H * SEG].rearrange("a (h t) -> (a h) t", t=SEG), row_y[j][:, :]).then_inc(x1_stored[j], 16)

            def rows(g, seg):
                for j in range(SLOTS):
                    n = g * SLOTS + j
                    load_row(n, j, seg, n if seg == 0 else n - B)
                    if not (isinstance(n, int) and n < 2):
                        of = seg if not (isinstance(n, int) and n - 2 < B) else 0
                        store_row(n - 2, (j + 2) % SLOTS, of, n - 2 if of == 0 else n - 2 - B)

            def load_x1(seg, k, j, gd):
                if isinstance(k, int) and k % H == 0:
                    for i in range(SLOTS):
                        sp.wait_ge(x1_stored[i], 16 * (B // SLOTS) * (seg + 1))
                if not (isinstance(k, int) and k < SLOTS):
                    sp.wait_ge(x2_stored[j], gd * 16)
                sp.dma_start(tile[j], x1_dram[seg][:, bass.ds(k * SEG - seg * H * SEG, SEG)]).then_inc(x1_loaded[j], 16)

            def store_kernel(k, j):
                i = j % 2
                sp.wait_ge(k_ready, k + 1)
                sp.dma_start(k_dram[bass.ds(k, 1), :].rearrange("a (s w) -> (a s) w", w=P + CHUNK), k_pad[i][:, :]).then_inc(k_stored[i], 16)

            def load_toeplitz(seg, k, j, gd):
                if seg == 0:
                    sp.wait_ge(k_stored[j % 2], gd * 32 + (j // 2 + 1) * 16)
                else:
                    sp.wait_ge(y_made, k * NQ - 3 * NQ)
                skewed = k_dram[bass.ds(k - seg * H, 1), P:TOEP].rearrange("a (s w) -> (a s) w", w=P + CHUNK - 1)[:, 0:CHUNK]
                sp.dma_start(toep[j][:, :], skewed).then_inc(toep_loaded[j], 16)

            def store_x2(seg, k, j):
                sp.wait_ge(y_taken, k * NQ + NQ)
                sp.dma_start(out[:, bass.ds(k - seg * H, 1), seg * SEG:(seg + 1) * SEG].rearrange("b a t -> b (a t)"), tile[j]).then_inc(x2_stored[j], 16)

            def load_edge(k, j):
                i = j % 2
                if isinstance(k, int) and k < H + 2:
                    sp.wait_ge(edge_saved[i], 16 * (H // 2))
                else:
                    sp.wait_ge(y_made, k * NQ - NQ)
                sp.dma_start(edge[i][:, :], edge_dram[bass.ds(k - H, 1), :, :].rearrange("a n b -> (a n) b")).then_inc(edge_loaded[i], 16)

            def store_b(k, j):
                sp.wait_ge(b_half, k + 1)
                sp.dma_start(b_dram[bass.ds(k, 1), :, :].rearrange("a s n -> (a s) n"), b_whole[j % 2][:, :, :].rearrange("s a n -> s (a n)")).then_inc(b_stored[j % 2], 16)

            def load_b(k, j):
                if isinstance(k, int) and k < H + 2:
                    sp.wait_ge(b_stored[j % 2], 16 * (H // 2))
                else:
                    sp.wait_ge(b_ready, k - 1)
                sp.dma_start(b_whole[j % 2][:, :, :].rearrange("s a n -> s (a n)"), b_dram[bass.ds(k - H, 1), :, :].rearrange("a s n -> (a s) n")).then_inc(b_loaded[j % 2], 16)

            rows(0, 0)
            with sp.Fori(1, SETUP[-1] + 1) as g:
                rows(g, 0)
            sp.wait_ge(pads_zeroed, 2)
            for k in range(2):
                store_kernel(k, k)
                store_b(k, k)
            with sp.Fori(SETUP[-1] + 1, GROUPS) as g:
                rows(g, 0)
            for g in range(GROUPS, ROWS_FIRST // SLOTS):
                rows(g, 1)
            load_toeplitz(0, 0, 0, 0)
            sp.wait_ge(par_ready, 1)
            for k in range(2):
                load_x1(0, k, k, 0)
            for n in (ROWS_FIRST - 2, ROWS_FIRST - 1):
                store_row(n, n % SLOTS, 1, n - B)
            for n in range(ROWS_FIRST, ROWS_FIRST + 3):
                load_row(n, n % SLOTS, 1, n - B)

            def channels(g, seg, with_rows):
                for j in range(SLOTS):
                    k = g * SLOTS + j
                    after, then, third = (later(g, j, seg, d) for d in (1, 2, 3))
                    j1, j2, j3 = ((j + d) % SLOTS for d in (1, 2, 3))
                    if after and after[0] == 0:
                        load_toeplitz(0, k + 1, j1, after[2])
                    if then:
                        load_x1(then[0], then[1], j2, then[2])
                    if then and then[0] == 1:
                        load_toeplitz(1, k + 2, j2, then[2])
                    if third and third[0] == 1:
                        load_b(k + 3, j3)
                    if with_rows and not (isinstance(g, int) and k + 3 >= B - AHEAD):
                        load_row(k + ROWS_FIRST + 3, j3, 1, k + AHEAD + 3)
                    if then and then[0] == 0:
                        store_kernel(k + 2, j2)
                        store_b(k + 2, j2)
                    if with_rows:
                        store_row(k + ROWS_FIRST, j, 1, k + AHEAD)
                    if seg == 0:
                        sp.wait_ge(s_ready, states_before(0, k) + NCH)
                        sp.dma_start(edge_dram[bass.ds(k, 1), :, :].rearrange("a n b -> (a n) b"), edge[j % 2][:, :]).then_inc(edge_saved[j % 2], 16)
                    if then and then[0] == 1:
                        load_edge(k + 2, j2)
                    store_x2(seg, k, j)

            channel_groups(sp, channels)
            for j in range(SLOTS):
                sp.wait_ge(x2_stored[j], 16 * NSEG * GROUPS)

        @block.gpsimd
        def _(pool):
            done = [0]

            def link(ins):
                done[0] += 1
                ins.then_inc(pool_step, 1)
                pool.wait_ge(pool_step, done[0])

            for i in range(2):
                pool.memset(k_pad[i][:, 0:P], 0.0).then_inc(pads_zeroed, 1)
            pool.iota(step_i, [[1, T]], base=0, channel_multiplier=0).then_inc(steps_made, 1)
            pool.wait_ge(turned_kept, 2)
            pool.wait_ge(consts_in, 16 * (NSETUP + 1))
            pool.wait_ge(w_in, 32)

            def bc(ap, k):
                return ap.unsqueeze(2).to_broadcast([P, HS, k])

            for q in range(H // HS):
                hs = slice(q * HS, (q + 1) * HS)
                w, r = tg[0][:, :, :], tg[1][:, :, :]
                link(pool.tensor_tensor(w, bc(f_t[:, hs], NTRIG), tau.unsqueeze(1).to_broadcast([P, HS, NTRIG]), ALU.mult))
                for last in (False, True):
                    link(pool.tensor_scalar(r, w, ROUND, -ROUND, ALU.add, ALU.add))
                    if last:
                        link(pool.tensor_tensor(table[:, hs, 0:NTRIG], w, r, ALU.subtract))
                    else:
                        link(pool.tensor_tensor(w, w, r, ALU.subtract))
                        link(pool.tensor_tensor(w, w, off.unsqueeze(1).to_broadcast([P, HS, NTRIG]), ALU.add))
                pool.sem_inc(sin_arg, 1)
            pool.wait_ge(sin_done, 2)
            pool.wait_ge(decay_done, 1)
            for q in range(H // HS):
                hs = slice(q * HS, (q + 1) * HS)
                for col, k0, k in ((COL_P1, 0, HIGH), (COL_P2, 0, HIGH), (COL_Q1, HIGH, LOW), (COL_Q2, HIGH, LOW)):
                    link(pool.tensor_tensor(table[:, hs, col:col + k], table[:, hs, col:col + k], decay[:, hs, k0:k0 + k], ALU.mult))
            re, im, top = slice(0, N), slice(N, P), HIGH - 1
            link(pool.tensor_copy(table[re, :, COL_RD], table[re, :, COL_P1 + top]))
            link(pool.tensor_scalar(table[im, :, COL_RD], table[im, :, COL_P2 + top], -1.0, None, ALU.mult))
            link(pool.tensor_scalar(table[re, :, COL_RO], table[re, :, COL_P2 + top], -1.0, None, ALU.mult))
            link(pool.tensor_copy(table[im, :, COL_RO], table[im, :, COL_P1 + top]))
            link(pool.tensor_scalar(table[:, :, COL_DP], d_bc[:, :], 1.0, None, ALU.add))

            def make_e(seg, k, j):
                if not (isinstance(k, int) and k < SLOTS):
                    pool.wait_ge(y_made, k * NQ - 3 * NQ)
                    pool.wait_ge(e_ready, e_before(seg, k))
                pool.tensor_copy(par[j][:, :], table[:, bass.ds(k - seg * H, 1), :].rearrange("p a k -> p (a k)")).then_inc(par_ready, 1)
                pool.wait_ge(par_ready, k + 1)
                for n, (p0, q0) in enumerate(((COL_P1, COL_Q1), (COL_P2, COL_Q2))):
                    pool.tensor_tensor(outer[:, n, :].rearrange("p (a b) -> p a b", b=LOW),
                                       par[j][:, p0:p0 + LOW].unsqueeze(2).to_broadcast([P, LOW, LOW]),
                                       par[j][:, q0:q0 + LOW].unsqueeze(1).to_broadcast([P, LOW, LOW]),
                                       ALU.mult).then_inc(e_ready, 1)
                pool.wait_ge(e_ready, e_before(seg, k) + 2)
                pool.tensor_tensor(e_mat[j][:, :], outer[:, 0, :], outer[:, 1, :], ALU.add).then_inc(e_ready, 1)
                if seg == 0:
                    pool.tensor_tensor(e_rev[j % 2][:, :], outer[:, 0, CHUNK - 1::-1], outer[:, 1, CHUNK - 1::-1], ALU.add).then_inc(e_ready, 1)

            for k in range(SLOTS):
                if k:
                    pool.wait_ge(e_ready, k * 4)
                if k == 2:
                    pool.wait_ge(gen_made, 1)
                if k == 3:
                    pool.wait_ge(gen_made, 2)
                make_e(0, k, k)

            def split_row(m, j):
                i = j % 2
                pool.wait_ge(row_halved, m + 1)
                pool.tensor_tensor(w_lo[i][:, :], w_sel[j][:, :], w_hi[i][:, :].bitcast(fp32), ALU.subtract)
                pool.tensor_tensor(x_lo[i][:, :], row_x[j][:, :], x_hi[i][:, :].bitcast(fp32), ALU.subtract).then_inc(row_split, 1)

            for m in range(2):
                split_row(m, m)

            def channels(g, with_rows):
                for j in range(SLOTS):
                    make_e(0, g * SLOTS + j, j)
                    if with_rows or j < 2:
                        split_row(g * SLOTS + (j - 2), (j + 2) % SLOTS)

            with pool.Fori(1, ROW_GROUPS) as g:
                channels(g, True)
            for g in range(ROW_GROUPS, GROUPS):
                channels(g, False)
            with pool.Fori(GROUPS, NSEG * GROUPS) as g:
                for j in range(SLOTS):
                    make_e(1, g * SLOTS + j, j)

        @block.scalar
        def _(act):
            def base_sines():
                act.wait_ge(base_arg, 1)
                nc.scalar.activation(trig_out[:, :, :], trig_arg[:, :, :], ACT.Sin, scale=SIN_SCALE).then_inc(base_trig, 1)

            def pick_w(n, j):
                if isinstance(n, int) and n == 0:
                    act.wait_ge(w_ready, 1)
                if not (isinstance(n, int) and n < SLOTS):
                    act.wait_ge(row_made, n * NQ - (SLOTS - 1) * NQ)
                which = act.value_load(cond_sb[0:1, bass.ds(n, 1)], min_val=0, max_val=NCOND - 1)
                nc.scalar.activation(w_sel[j][:, :], w_all[:, bass.ds(which, 1), :].rearrange("c k d -> c (k d)"), ACT.Copy).then_inc(w_picked, 1)

            def halve_x(m, j, q):
                i, n, cols = j % 2, m + ROWS_FIRST, slice(q * BANK, (q + 1) * BANK)
                if q == 0:
                    act.wait_ge(x_loaded[j], n * 4 + (16 - j * 4))
                ins = nc.scalar.activation(x_hi[i][:, cols], row_x[j][:, cols], ACT.Copy)
                if q == NQ - 1:
                    ins.then_inc(row_halved, 1)

            def halve_w(m, j):
                n = m + ROWS_FIRST
                act.wait_ge(row_made, n * NQ - NQ)
                which = act.value_load(cond_sb[0:1, bass.ds(n, 1)], min_val=0, max_val=NCOND - 1)
                w = w_all[:, bass.ds(which, 1), :].rearrange("c k d -> c (k d)")
                nc.scalar.activation(w_sel[j][:, :], w, ACT.Copy)
                nc.scalar.activation(w_hi[j % 2][:, :], w, ACT.Copy)

            def take_row(n, j, q, from_bank):
                if q == 0 and not (isinstance(n, int) and n < SLOTS):
                    act.wait_ge(x1_stored[j], n * 4 - j * 4)
                act.wait_ge(row_made, n * NQ + (q + 1))
                nc.scalar.activation(row_y[j][:, q * BANK:(q + 1) * BANK], from_bank[:, :], ACT.Copy).then_inc(row_taken, 1)

            def rows(g):
                for j in range(SLOTS):
                    for q in range(NQ):
                        take_row(g * SLOTS + j, j, q, bank[(j % 2) * NQ + q])
                        if q == 0:
                            pick_w(g * SLOTS + (j + 1), (j + 1) % SLOTS)

            def keep_parameters():
                act.wait_ge(turned_done, 5)
                for n, dst in enumerate((ar_t[:, :], f_t[:, :], table[:, :, COL_S1], table[:, :, COL_S2])):
                    last = nc.scalar.activation(dst, bank[4][:, n * P:(n + 1) * P], ACT.Copy)
                last.then_inc(turned_kept, 1)
                nc.scalar.activation(table[:, :, COL_CK], bank[5][:, 0:P], ACT.Copy).then_inc(turned_kept, 1)

            def make_sines(half):
                act.wait_ge(sin_arg, H // HS)
                part = table[:, half * (H // 2):(half + 1) * (H // 2), 0:NTRIG]
                nc.scalar.activation(part, part, ACT.Sin, scale=SIN_SCALE).then_inc(sin_done, 1)

            def keep_b(seg, k, j):
                i = j % 2
                if seg == 0:
                    act.wait_ge(gen_made, k + 1)
                    act.wait_ge(k_ready, k + 1)
                    if not (isinstance(k, int) and k < 2):
                        act.wait_ge(b_stored[i], k * 8 - i * 8)
                    nc.scalar.activation(b_whole[i][:, :, :], b_part, ACT.Copy)
                else:
                    act.wait_ge(b_loaded[i], k * 8 + (16 - i * 8 - 8 * H))
                nc.scalar.activation(b_hi[j][:, :, :], b_part if seg == 0 else b_whole[i][:, :, :], ACT.Copy).then_inc(b_half, 1)

            def halve_e(seg, k, j):
                act.wait_ge(e_ready, e_before(seg, k) + 3)
                nc.scalar.activation(e_hi[j][:, :], e_mat[j][:, :], ACT.Copy).then_inc(e_half, 1)

            def first_matrices(k):
                for e in ((0, 1), (2,))[k]:
                    halve_e(0, e, e)
                keep_b(0, k, k)

            act.wait_ge(consts_in, 16 * (NSETUP + 1))
            pick_w(0, 0)
            row_groups(act, rows, base_sines, keep_parameters, lambda: make_sines(0), lambda: make_sines(1), lambda: first_matrices(0), lambda: first_matrices(1))

            def keep_u(k, j, q):
                act.wait_ge(u_made, k * NQ + (q + 1))
                blocks = t_bank[q][:, :].rearrange("s (k b) -> s k b", b=B)
                nc.scalar.activation(u_odd[j % 2][:, 2 * q:2 * q + 2, :], blocks[:, 1::2, :], ACT.Copy)
                nc.scalar.activation(u_hi[j % 2][:, 4 * q:4 * q + 4, :], blocks, ACT.Copy).then_inc(u_half, 1)

            def keep_s(seg, k, j, c):
                made = states_before(seg, k) + c
                act.wait_ge(s_made, made)
                if c == NCH and not (isinstance(k, int) and k < 2):
                    act.wait_ge(edge_saved[j % 2], k * 8 - j % 2 * 8)
                dst = edge[j % 2] if c == NCH else state[c]
                nc.scalar.activation(dst[:, :], s_bank[j % 2][:, (c - 1) * P:c * P], ACT.Copy).then_inc(s_ready, 1)
                if c < NCH:
                    act.wait_ge(s_ready, made)
                    nc.scalar.activation(s_hi[c][:, :], state[c][:, :], ACT.Copy).then_inc(s_half, 1)

            def halve_edge(k, j, gd):
                act.wait_ge(edge_loaded[j % 2], gd * 32 + (j // 2 + 1) * 16 - 16 * H // 2)
                act.wait_ge(y_made, k * NQ)
                nc.scalar.activation(s_hi[0][:, :], edge[j % 2][:, :], ACT.Copy).then_inc(s_half, 1)

            def halve_toeplitz(j, gd):
                act.wait_ge(toep_loaded[j], gd * 16 + 16)
                nc.scalar.activation(t_hi[j][:, :], toep[j][:, :], ACT.Copy).then_inc(toep_half, 1)

            for q in range(NQ):
                keep_u(0, 0, q)
            halve_toeplitz(0, 0)
            halve_w(0, 0)
            for q in range(NQ):
                halve_x(0, 0, q)

            def channels(g, seg, with_rows):
                for j in range(SLOTS):
                    k = g * SLOTS + j
                    j1, j2 = (j + 1) % SLOTS, (j + 2) % SLOTS
                    after, then, third = (later(g, j, seg, d) for d in (1, 2, 3))
                    if seg == 1:
                        halve_edge(k, j, g)
                    next_row = with_rows and not (isinstance(g, int) and k + 1 >= B - AHEAD)
                    keep_s(seg, k, j, 1)
                    if next_row:
                        halve_w(k + 1, j1)
                        halve_x(k + 1, j1, 0)
                    if after:
                        keep_u(k + 1, j1, 0)
                    keep_s(seg, k, j, 2)
                    if after:
                        keep_u(k + 1, j1, 1)
                    keep_s(seg, k, j, 3)
                    if with_rows:
                        take_row(k + ROWS_FIRST, j, 0, row_bank)
                    if next_row:
                        halve_x(k + 1, j1, 1)
                    if after:
                        halve_toeplitz(j1, after[2])
                    if then:
                        keep_b(then[0], k + 2, j2)
                    if third:
                        halve_e(third[0], k + 3, (j + 3) % SLOTS)
                    if seg == 0:
                        keep_s(seg, k, j, NCH)
                    if with_rows:
                        take_row(k + ROWS_FIRST, j, 1, row_bank)

            channel_groups(act, channels)

        @block.vector
        def _(dve):
            done = [0]

            def link(ins):
                done[0] += 1
                ins.then_inc(dve_step, 1)
                dve.wait_ge(dve_step, done[0])

            v = nc.vector
            dve.wait_ge(w_in, 32)
            v.tensor_tensor(w_all[:, :, :], w_all[:, :, :], eye.unsqueeze(1).to_broadcast([P, NCOND, P]), ALU.add).then_inc(w_ready, 1)
            dve.wait_ge(consts_in, 16 * (NSETUP + 1))
            link(v.tensor_copy(len_f[:, :], len_i[:, :]))
            (are, ar, ai, k, r, t, er, xr, xi, nr, den, rd, qr, qi, c2r, c2i, lr, li, w0, w1, w2) = (base[:, n, :] for n in range(21))
            e5 = [e[:, 0:N + 1] for e in ex]
            link(v.tensor_copy(e5[0], logs[:, :]))
            exp_steps(v, link, exps[:, :], e5[0:4], ex_i[:, 0:N + 1])
            dt = exps[:, N:N + 1]
            link(v.tensor_scalar(are, exps[:, 0:N], -1.0, None, ALU.mult))
            link(v.tensor_scalar(ar, are, dt, None, ALU.mult))
            link(v.tensor_scalar(ai, aim[:, :], dt, None, ALU.mult))
            link(v.tensor_scalar(k, ai, INV_2PI, ROUND, ALU.mult, ALU.add))
            link(v.tensor_scalar(k, k, -ROUND, None, ALU.add))
            link(v.tensor_copy(r, ai))
            for part in TWO_PI:
                link(v.scalar_tensor_tensor(r, k, -part, r, ALU.mult, ALU.add))
            link(v.tensor_scalar(trig_arg[:, 0, :], r, INV_2PI, None, ALU.mult))
            link(v.tensor_scalar(w0, trig_arg[:, 0, :], 0.25, None, ALU.add))
            link(v.tensor_scalar(w1, w0, ROUND, -ROUND, ALU.add, ALU.add))
            v.tensor_tensor(trig_arg[:, 1, :], w0, w1, ALU.subtract).then_inc(base_arg, 1)
            e4 = [e[:, 0:N] for e in ex]
            link(v.tensor_copy(e4[0], ar))
            exp_steps(v, link, er, e4[0:4], ex_i[:, 0:N])
            dve.wait_ge(base_trig, 1)
            link(v.tensor_tensor(xr, er, trig_out[:, 1, :], ALU.mult))
            link(v.tensor_tensor(xi, er, trig_out[:, 0, :], ALU.mult))
            link(v.tensor_scalar(nr, xr, -1.0, None, ALU.add))
            link(v.tensor_tensor(w0, are, are, ALU.mult))
            link(v.tensor_tensor(w1, aim[:, :], aim[:, :], ALU.mult))
            link(v.tensor_tensor(den, w0, w1, ALU.add))
            link(v.reciprocal(rd, den))

            def complex_mult(o_re, o_im, a_re, a_im, b_re, b_im, conj=False):
                link(v.tensor_tensor(w0, a_re, b_re, ALU.mult))
                link(v.tensor_tensor(w1, a_im, b_im, ALU.mult))
                link(v.tensor_tensor(o_re, w0, w1, ALU.add if conj else ALU.subtract))
                link(v.tensor_tensor(w0, a_im, b_re, ALU.mult))
                link(v.tensor_tensor(w1, a_re, b_im, ALU.mult))
                link(v.tensor_tensor(o_im, w0, w1, ALU.subtract if conj else ALU.add))

            complex_mult(qr, qi, nr, xi, are, aim[:, :], conj=True)
            link(v.tensor_tensor(qr, qr, rd, ALU.mult))
            link(v.tensor_tensor(qi, qi, rd, ALU.mult))
            complex_mult(c2r, c2i, c_sb[:, :, 0], c_sb[:, :, 1], qr, qi)
            link(v.tensor_scalar(c2r, c2r, 2.0, None, ALU.mult))
            link(v.tensor_scalar(c2i, c2i, 2.0, None, ALU.mult))
            complex_mult(lr, li, c2r, c2i, xr, xi)
            for n, (one, two) in enumerate(((ar, ar), (trig_arg[:, 0, :], trig_arg[:, 0, :]), (lr, lr), (li, li), (c2r, c2i))):
                link(v.tensor_copy(turned[:, n, 0:N], one))
                if n == 2:
                    link(v.tensor_scalar(turned[:, n, N:P], two, -1.0, None, ALU.mult))
                elif n < 4:
                    link(v.tensor_copy(turned[:, n, N:P], two))
                else:
                    v.tensor_copy(turned[:, n, N:P], two).then_inc(base_done, 1)
            dve.wait_ge(steps_made, 1)
            link(v.tensor_scalar(mask[:, :], step_i, len_f[:, 0:1], None, ALU.is_lt))

            dve.wait_ge(turned_kept, 1)
            for q in range(H // HS):
                hs = slice(q * HS, (q + 1) * HS)
                link(v.tensor_tensor(ex[0][:, :].rearrange("p (h k) -> p h k", k=NEXP), ar_t[:, hs].unsqueeze(2).to_broadcast([P, HS, NEXP]),
                                     tau_exp.unsqueeze(1).to_broadcast([P, HS, NEXP]), ALU.mult))
                exp_steps(v, link, decay_cols[:, q * HS * NEXP:(q + 1) * HS * NEXP], [e[:, :] for e in ex[0:4]], ex_i[:, :])
            dve.sem_inc(decay_done, 1)

            def mats(seg, k, j):
                i, p = j % 2, par[j]
                dve.wait_ge(par_ready, k + 1)
                if seg == 0 and not (isinstance(k, int) and k < 2):
                    dve.wait_ge(gen_made, k - 1)
                if not (isinstance(k, int) and k < 4):
                    dve.wait_ge(y_made, k * NQ - 3 * NQ)
                v.tensor_scalar(r_tmp[i][:, :], eye, p[:, COL_RD:COL_RD + 1], None, ALU.mult).then_inc(mats_ready, 1)
                if seg == 0:
                    v.tensor_scalar(m_tmp[i][:, :], eye, p[:, COL_S1:COL_S1 + 1], None, ALU.mult).then_inc(mats_ready, 1)
                    v.tensor_scalar(ck_hi[i][:, :], ones, p[:, COL_CK:COL_CK + 1], None, ALU.mult).then_inc(mats_ready, 1)
                dve.wait_ge(mats_ready, mats_before(seg, k) + (3 if seg == 0 else 1))
                v.scalar_tensor_tensor(r_mat[j][:, :], swap, p[:, COL_RO:COL_RO + 1], r_tmp[i][:, :], ALU.mult, ALU.add).then_inc(mats_ready, 1)
                if seg == 0:
                    v.scalar_tensor_tensor(ck_lo[i][:, :], ones, p[:, COL_CK:COL_CK + 1], ck_hi[i][:, :].bitcast(fp32), ALU.mult, ALU.subtract).then_inc(mats_ready, 1)
                    v.scalar_tensor_tensor(m_mat[i][:, :], swap, p[:, COL_S2:COL_S2 + 1], m_tmp[i][:, :], ALU.mult, ALU.add).then_inc(mats_ready, 1)

            def keep_k(k, j):
                i = j % 2
                dve.wait_ge(gen_made, k + 1)
                if not (isinstance(k, int) and k < 2):
                    dve.wait_ge(k_stored[i], k * 8 - i * 8)
                v.scalar_tensor_tensor(k_pad[i][:, P:P + CHUNK], delta, par[j][:, COL_DP:COL_DP + 1], k_part, ALU.mult, ALU.add).then_inc(k_ready, 1)

            def split_b(seg, k, j):
                dve.wait_ge(b_half, k + 1)
                v.tensor_tensor(b_lo[j][:, :, :], b_part if seg == 0 else b_whole[j % 2][:, :, :], b_hi[j][:, :, :].bitcast(fp32), ALU.subtract).then_inc(b_ready, 1)

            def split_e(k, j):
                dve.wait_ge(e_half, k + 1)
                v.tensor_tensor(e_lo[j][:, :], e_mat[j][:, :], e_hi[j][:, :].bitcast(fp32), ALU.subtract).then_inc(e_split, 1)

            def split_toeplitz(k, j):
                dve.wait_ge(toep_half, k + 1)
                v.tensor_tensor(t_lo[j][:, :], toep[j][:, :], t_hi[j][:, :].bitcast(fp32), ALU.subtract).then_inc(toep_split, 1)

            def split_u(k, j, q):
                dve.wait_ge(u_half, k * NQ + (q + 1))
                blocks = slice(4 * q, 4 * q + 4)
                v.tensor_tensor(u_lo[j % 2][:, blocks, :], t_bank[q][:, :].rearrange("s (k b) -> s k b", b=B),
                                u_hi[j % 2][:, blocks, :].bitcast(fp32), ALU.subtract).then_inc(u_ready, 1)

            def split_s(seg, k, j, c):
                dve.wait_ge(s_half, splits_before(seg, k) + (c + seg))
                whole = edge[j % 2] if c == 0 else state[c]
                v.tensor_tensor(s_lo[c][:, :], whole[:, :], s_hi[c][:, :].bitcast(fp32), ALU.subtract).then_inc(s_split, 1)

            def take_y(seg, k, j, q):
                dve.wait_ge(y_made, k * NQ + (q + 1))
                dve.sem_inc(y_seen, 1)
                cols = slice(q * BANK, (q + 1) * BANK)
                v.copy_predicated(tile[j][:, cols], mask[:, seg * SEG + q * BANK:seg * SEG + (q + 1) * BANK], y_bank[q][:, :]).then_inc(y_taken, 1)

            dve.wait_ge(pads_zeroed, 2)
            for k in range(2):
                mats(0, k, k)
                split_e(k, k)
            for k in range(2):
                keep_k(k, k)
                split_b(0, k, k)
                if k == 0:
                    mats(0, 2, 2)
                    split_e(2, 2)
            for q in range(NQ):
                split_u(0, 0, q)
            split_toeplitz(0, 0)

            def channels(g, seg, with_rows):
                for j in range(SLOTS):
                    k = g * SLOTS + j
                    j1, j2 = (j + 1) % SLOTS, (j + 2) % SLOTS
                    after, then = later(g, j, seg, 1), later(g, j, seg, 2)
                    if seg == 1:
                        split_s(seg, k, j, 0)
                    split_s(seg, k, j, 1)
                    third = later(g, j, seg, 3)
                    if third:
                        mats(third[0], k + 3, (j + 3) % SLOTS)
                    if after:
                        split_u(k + 1, j1, 0)
                    if then and then[0] == 0:
                        keep_k(k + 2, j2)
                    split_s(seg, k, j, 2)
                    if after:
                        split_u(k + 1, j1, 1)
                    split_s(seg, k, j, 3)
                    if after:
                        split_toeplitz(k + 1, j1)
                    take_y(seg, k, j, 0)
                    if then:
                        split_b(then[0], k + 2, j2)
                    if third:
                        split_e(k + 3, (j + 3) % SLOTS)
                    take_y(seg, k, j, 1)

            channel_groups(dve, channels)

        @block.tensor
        def _(pe):
            mm = nc.tensor.matmul
            pe.wait_ge(w_in, 32)

            def turn_parameters():
                pe.wait_ge(base_done, 1)
                for n in range(5):
                    nc.tensor.transpose(bank[4 + n // 4][:, (n % 4) * P:(n % 4 + 1) * P], turned[:, n, :], eye).then_inc(turned_done, 1)

            def row_product(n, j, q, to_bank):
                if q == 0:
                    pe.wait_ge(x_loaded[j], n * 4 + (16 - j * 4))
                    pe.wait_ge(w_picked, n + 1)
                if not (isinstance(n, int) and n < 2):
                    pe.wait_ge(row_taken, n * NQ + (q + 1 - 2 * NQ))
                mm(to_bank[:, :], w_sel[j][:, :], row_x[j][:, q * BANK:(q + 1) * BANK], start=True, stop=True).then_inc(row_made, 1)

            def rows(g):
                for j in range(SLOTS):
                    for q in range(NQ):
                        row_product(g * SLOTS + j, j, q, bank[(j % 2) * NQ + q])

            def turn(k, j, q):
                if not (isinstance(k, int) and k == 0):
                    pe.wait_ge(u_ready, k * NQ + (q - 1))
                for n in range(4):
                    at = (4 * q + n) * P
                    ins = nc.tensor.transpose(t_bank[q][:, n * P:(n + 1) * P], tile[j][:, at:at + P], eye)
                ins.then_inc(u_made, 1)

            def make_mats(k, j):
                i = j % 2
                pe.wait_ge(e_ready, e_before(0, k) + 4)
                pe.wait_ge(mats_ready, mats_before(0, k) + 6)
                pe.wait_ge(e_split, k + 1)
                if not (isinstance(k, int) and k == 0):
                    pe.wait_ge(b_ready, k)
                split_mm(k_part, ck_hi[i][:, :], ck_lo[i][:, :], e_hi[j][:, :], e_lo[j][:, :], start=True, stop=True)
                for p in range(2):
                    ins = mm(b_part[:, p, :], e_rev[i][:, p * P:(p + 1) * P], m_mat[i][:, :], start=True, stop=True)
                ins.then_inc(gen_made, 1)

            def split_mm(to, w_hi, w_lo, m_hi, m_lo, start, stop):
                mm(to, w_hi, m_hi, start=start, stop=False, skip_group_check=True)
                mm(to, w_hi, m_lo, start=False, stop=False, skip_group_check=True)
                return mm(to, w_lo, m_hi, start=False, stop=stop, skip_group_check=True)

            def row_in_parts(m, j, q):
                i, cols = j % 2, slice(q * BANK, (q + 1) * BANK)
                if q == 0:
                    pe.wait_ge(row_split, m + 1)
                pe.wait_ge(row_taken, m * NQ + (ROWS_FIRST * NQ + q))
                split_mm(row_bank[:, :], w_hi[i][:, :], w_lo[i][:, :], x_hi[i][:, cols], x_lo[i][:, cols], start=True, stop=True).then_inc(row_made, 1)

            def drive(seg, k, j):
                i, n = j % 2, NCH - seg
                pe.wait_ge(b_ready, k + 1)
                pe.wait_ge(u_ready, k * NQ + NQ)
                if not (isinstance(k, int) and k < 2):
                    pe.wait_ge(s_ready, states_before(seg, k - 1))
                u = [a[i][:, :, :].rearrange("s (c p) b -> s c p b", p=2)[:, 0:n, :, :] for a in (u_hi, u_lo)]
                for p in range(2):
                    ins = split_mm(s_bank[i][:, 0:n * P], b_hi[j][:, p, :], b_lo[j][:, p, :], u[0][:, :, p, :], u[1][:, :, p, :],
                                   start=(p == 0), stop=(p == 1))
                if seg == 0:
                    ins.then_inc(s_made, 1)

            def advance(seg, k, j, c):
                if c == 0:
                    pe.wait_ge(edge_loaded[j % 2], k * 8 + (16 - j % 2 * 8 - 8 * H))
                    whole = edge[j % 2]
                else:
                    pe.wait_ge(s_ready, states_before(seg, k) + c)
                    whole = state[c]
                mm(s_bank[j % 2][:, c * P:(c + 1) * P], r_mat[j][:, :], whole[:, :], start=False, stop=True, skip_group_check=True).then_inc(s_made, 1)

            def chunk_columns(c):
                return y_bank[c // 2][:, (c % 2) * CHUNK:(c % 2 + 1) * CHUNK]

            def from_chunk(k, j, c):
                i, y = j % 2, chunk_columns(c)
                split_mm(y, u_hi[i][:, 2 * c, :], u_lo[i][:, 2 * c, :], t_hi[j][:, :], t_lo[j][:, :], start=(c % 2 == 0), stop=False)
                mm(y[:, P:CHUNK], u_odd[i][:, c, :], toep[j][:, 0:P], start=False, stop=True, skip_group_check=True)

            def from_state(seg, k, j, c):
                pe.wait_ge(s_split, splits_before(seg, k) + (c + seg))
                ins = split_mm(chunk_columns(c), s_hi[c][:, :], s_lo[c][:, :], e_hi[j][:, :], e_lo[j][:, :], start=False, stop=True)
                if c % 2:
                    ins.then_inc(y_made, 1)

            def channels(g, seg, with_rows):
                for j in range(SLOTS):
                    k = g * SLOTS + j
                    j1, j2 = (j + 1) % SLOTS, (j + 2) % SLOTS
                    after, then = later(g, j, seg, 1), later(g, j, seg, 2)
                    drive(seg, k, j)
                    if seg == 1:
                        pe.wait_ge(mats_ready, mats_before(1, k) + 2)
                    pe.wait_ge(toep_split, k + 1)
                    pe.wait_ge(e_split, k + 1)
                    for c in range(NCH):
                        if c >= 1 - seg and c < NCH - seg:
                            advance(seg, k, j, c)
                        if c % 2 == 0 and not (isinstance(k, int) and k == 0):
                            pe.wait_ge(y_taken, k * NQ + (c // 2 - 1))
                        from_chunk(k, j, c)
                        if c - 1 >= 1 - seg:
                            from_state(seg, k, j, c - 1)
                        if c == 0 and after:
                            pe.wait_ge(x1_loaded[j1], after[2] * 16 + 16)
                            for q in range(NQ):
                                turn(k + 1, j1, q)
                        if c == 0 and then and then[0] == 0:
                            make_mats(k + 2, j2)
                        if with_rows and c % 2:
                            row_in_parts(k, j, c // 2)
                    from_state(seg, k, j, NCH - 1)

            row_groups(pe, rows, None, turn_parameters, None, None, lambda: make_mats(0, 0), lambda: make_mats(1, 1))
            pe.wait_ge(turned_kept, 2)
            pe.wait_ge(row_taken, ROWS_FIRST * NQ)
            pe.wait_ge(x1_loaded[0], 16)
            for q in range(NQ):
                turn(0, 0, q)
            channel_groups(pe, channels)


_INS = ["x", "itok_B_0_15", "itok_B_8_3872", "L0_cond_weights", "L1_cond_log_dt", "L1_cond_C",
        "L1_cond_log_A_real", "L1_cond_A_imag", "L1_cond_D"]


def _constants(np):
    c = np.zeros((P, NCONST), np.float32)
    rows = np.arange(P)
    c[rows, C_EYE + rows] = 1.0
    c[rows, C_SWAP + (rows + N) % P] = 1.0
    c[:, C_ONES:C_ONES + P] = 1.0
    high, low = 16.0 * np.arange(HIGH), np.arange(LOW)
    c[:, C_TAU:C_TAU + NTRIG] = np.concatenate([high, high, low, low])
    imag = (rows >= N)[:, None] * 0.25
    o = np.concatenate([np.full(HIGH, 0.25), np.full(HIGH, 0.5), np.full(LOW, 0.25), np.zeros(LOW)])
    c[:, C_OFF:C_OFF + NTRIG] = o + imag * (np.arange(NTRIG) < 2 * HIGH)
    c[:, C_EXP:C_EXP + NEXP] = np.concatenate([high, low])
    c[:, C_DELTA] = 1.0
    return c


def kernel(**inputs):
    import numpy as np
    import concourse.bacc as bacc
    from concourse.bass_utils import run_bass_kernel_spmd

    nc = bacc.Bacc("TRN2", target_bir_lowering=False, num_devices=1)
    arrays, args = {}, []
    for name, a in [(n, np.ascontiguousarray(inputs[n])) for n in _INS] + [("constants", _constants(np))]:
        arrays[f"in_{name}"] = a
        args.append(nc.dram_tensor(f"in_{name}", a.shape, mybir.dt.from_np(a.dtype), kind="ExternalInput").ap())
    out = nc.dram_tensor("out_0", (B, H, T), mybir.dt.float32, kind="ExternalOutput").ap()
    s4d_program(nc, *args[:9], args[9], out)
    r = run_bass_kernel_spmd(nc, [arrays], core_ids=[0])
    return r.results[0]["out_0"]
```
